# Optimizing a Trainium2 kernel written in Bass

```python
import numpy as np
import jax
import jax.numpy as jnp

def _softmax(x, axis=-1):
    return jax.nn.softmax(x, axis=axis)

def _gelu(x):
    return jax.nn.gelu(x, approximate=True)

def _silu(x):
    return jax.nn.silu(x)

def _sigmoid(x):
    return jax.nn.sigmoid(x)

def _layernorm(x, axis=-1, eps=1e-05):
    m = jnp.mean(x, axis=axis, keepdims=True)
    v = jnp.var(x, axis=axis, keepdims=True)
    return (x - m) / jnp.sqrt(v + eps)

def _scatter_add(tgt, idx, src, axis=0):
    return tgt.at[idx].add(src)

def _segment_sum(src, seg, n):
    return jax.ops.segment_sum(src, seg, n)
kernel_name = 'mk_xattn_seq_d2_seqx_r8_60ec42'

def setup_inputs(seed: int=0):
    np.random.seed(seed)
    _w = jnp.asarray

    def _rec_inputs():
        import jax
        import jax.numpy as jnp
        _rk = jax.random.key(seed)
        x = -0.0003929 + 0.9999 * jax.random.normal(jax.random.fold_in(_rk, 1), (8, 256, 256), jnp.float32)
        _lenS = 256 - jax.random.randint(jax.random.fold_in(_rk, 7), (8,), 0, max(1, 256 // 4) + 1, jnp.int32)
        _lenS2 = 1601 - jax.random.randint(jax.random.fold_in(_rk, 8), (8,), 0, max(1, 1601 // 4) + 1, jnp.int32)
        _ctx_2048P = jax.random.normal(jax.random.fold_in(_rk, 11), (8, 16, 256), jnp.float32)
        _ctx_2048c = jax.random.dirichlet(jax.random.fold_in(_rk, 511), 0.3 * jnp.ones((16,), jnp.float32), (8, 1601))
        _ctx_2048t = jnp.einsum('bsk,bkd->bsd', _ctx_2048c, _ctx_2048P)
        _ctx_2048t = _ctx_2048t * jax.lax.rsqrt(jnp.mean(jnp.square(_ctx_2048t)) + 1e-12) * 0.953939
        ctx_2048 = -8.57375e-05 + 0.999917 * (_ctx_2048t + 0.3 * jax.random.normal(jax.random.fold_in(_rk, 611), (8, 1601, 256), jnp.float32))
        _validS = jnp.arange(256)[None, :] < _lenS[:, None]
        _validS2 = jnp.arange(1601)[None, :] < _lenS2[:, None]
        _causal = jnp.tril(jnp.ones((256, 256), dtype=bool))
        mask_BxS2_bf1 = jnp.ones((8, 1601), dtype=bool)
        return (x, ctx_2048, mask_BxS2_bf1)
    x, ctx_2048, mask_BxS2_bf1 = _rec_inputs()

    def _L0_xattn_setup():
        import jax, jax.numpy as jnp
        import numpy as np
        HIDDEN = 256
        HEADS = 16
        HEAD_DIM = HIDDEN // HEADS
        LN_EPS = 1e-05
        GATE_INIT = 0.5

        def _layer_norm(x, gamma, beta):
            mu = jnp.mean(x, axis=-1, keepdims=True)
            var = jnp.mean(jnp.square(x - mu), axis=-1, keepdims=True)
            return (x - mu) * jax.lax.rsqrt(var + LN_EPS) * gamma + beta
        key = jax.random.key(seed)
        ks = jax.random.split(key, 8)
        B, T_TEXT, T_AUDIO = (4, 256, 1500)
        s = 0.02
        return {'hidden_states': jax.random.normal(ks[0], (B, T_TEXT, HIDDEN), jnp.float32), 'audio_kv': jax.random.normal(ks[1], (B, T_AUDIO, HIDDEN), jnp.float32), 'audio_attention_mask': jnp.ones((B, T_AUDIO), dtype=bool), 'Wq': jax.random.normal(ks[2], (HIDDEN, HIDDEN), jnp.float32) * s, 'Wk': jax.random.normal(ks[3], (HIDDEN, HIDDEN), jnp.float32) * s, 'Wv': jax.random.normal(ks[4], (HIDDEN, HIDDEN), jnp.float32) * s, 'Wo': jax.random.normal(ks[5], (HIDDEN, HIDDEN), jnp.float32) * s, 'ln_gamma': jnp.ones((HIDDEN,), jnp.float32), 'ln_beta': jnp.zeros((HIDDEN,), jnp.float32), 'gate': jnp.array([GATE_INIT], jnp.float32)}
    _L0_xattn_all = _L0_xattn_setup()
    _L0_xattn_in = {k: v for k, v in _L0_xattn_all.items() if k in ('Wq', 'Wk', 'Wv', 'Wo', 'ln_gamma', 'ln_beta', 'gate')}
    del _L0_xattn_all

    def _L1_xattn_setup():
        import jax, jax.numpy as jnp
        import numpy as np
        D = 256
        H = 16
        HD = D // H
        INNER = 4 * D
        EPS = 1e-05

        def layer_norm(x, w, b):
            mu = jnp.mean(x, axis=-1, keepdims=True)
            var = jnp.mean(jnp.square(x - mu), axis=-1, keepdims=True)
            return (x - mu) * jax.lax.rsqrt(var + EPS) * w + b
        key = jax.random.key(seed)
        ks = jax.random.split(key, 12)
        B, LQ, LK = (4, 128, 256)
        std = 0.02
        inp = {'hidden_states': jax.random.normal(ks[0], (B, LQ, D), jnp.float32), 'encoder_hidden_states': jax.random.normal(ks[1], (B, LK, D), jnp.float32), 'encoder_attention_mask': jnp.ones((B, LK), dtype=bool), 'ln1_w': jnp.ones((D,), jnp.float32), 'ln1_b': jnp.zeros((D,), jnp.float32), 'q_w': jax.random.normal(ks[2], (D, D), jnp.float32) * std, 'q_b': jnp.zeros((D,), jnp.float32), 'k_w': jax.random.normal(ks[3], (D, D), jnp.float32) * std, 'k_b': jnp.zeros((D,), jnp.float32), 'v_w': jax.random.normal(ks[4], (D, D), jnp.float32) * std, 'v_b': jnp.zeros((D,), jnp.float32), 'cproj_w': jax.random.normal(ks[5], (D, D), jnp.float32) * std, 'cproj_b': jnp.zeros((D,), jnp.float32), 'ln2_w': jnp.ones((D,), jnp.float32), 'ln2_b': jnp.zeros((D,), jnp.float32), 'fc_w': jax.random.normal(ks[6], (D, INNER), jnp.float32) * std, 'fc_b': jnp.zeros((INNER,), jnp.float32), 'proj_w': jax.random.normal(ks[7], (INNER, D), jnp.float32) * std, 'proj_b': jnp.zeros((D,), jnp.float32)}
        return inp
    _L1_xattn_all = _L1_xattn_setup()
    _L1_xattn_in = {k: v for k, v in _L1_xattn_all.items() if k in ('ln1_w', 'ln1_b', 'q_w', 'q_b', 'k_w', 'k_b', 'v_w', 'v_b', 'cproj_w', 'cproj_b', 'ln2_w', 'ln2_b', 'fc_w', 'fc_b', 'proj_w', 'proj_b')}
    del _L1_xattn_all
    return {'x': x, 'ctx_2048': ctx_2048, 'mask_BxS2_bf1': mask_BxS2_bf1, 'L0_xattn_Wq': _L0_xattn_in['Wq'], 'L0_xattn_Wk': _L0_xattn_in['Wk'], 'L0_xattn_Wv': _L0_xattn_in['Wv'], 'L0_xattn_Wo': _L0_xattn_in['Wo'], 'L0_xattn_ln_gamma': _L0_xattn_in['ln_gamma'], 'L0_xattn_ln_beta': _L0_xattn_in['ln_beta'], 'L0_xattn_gate': _L0_xattn_in['gate'], 'L1_xattn_ln1_w': _L1_xattn_in['ln1_w'], 'L1_xattn_ln1_b': _L1_xattn_in['ln1_b'], 'L1_xattn_q_w': _L1_xattn_in['q_w'], 'L1_xattn_q_b': _L1_xattn_in['q_b'], 'L1_xattn_k_w': _L1_xattn_in['k_w'], 'L1_xattn_k_b': _L1_xattn_in['k_b'], 'L1_xattn_v_w': _L1_xattn_in['v_w'], 'L1_xattn_v_b': _L1_xattn_in['v_b'], 'L1_xattn_cproj_w': _L1_xattn_in['cproj_w'], 'L1_xattn_cproj_b': _L1_xattn_in['cproj_b'], 'L1_xattn_ln2_w': _L1_xattn_in['ln2_w'], 'L1_xattn_ln2_b': _L1_xattn_in['ln2_b'], 'L1_xattn_fc_w': _L1_xattn_in['fc_w'], 'L1_xattn_fc_b': _L1_xattn_in['fc_b'], 'L1_xattn_proj_w': _L1_xattn_in['proj_w'], 'L1_xattn_proj_b': _L1_xattn_in['proj_b']}

def reference(x, ctx_2048, mask_BxS2_bf1, L0_xattn_Wq, L0_xattn_Wk, L0_xattn_Wv, L0_xattn_Wo, L0_xattn_ln_gamma, L0_xattn_ln_beta, L0_xattn_gate, L1_xattn_ln1_w, L1_xattn_ln1_b, L1_xattn_q_w, L1_xattn_q_b, L1_xattn_k_w, L1_xattn_k_b, L1_xattn_v_w, L1_xattn_v_b, L1_xattn_cproj_w, L1_xattn_cproj_b, L1_xattn_ln2_w, L1_xattn_ln2_b, L1_xattn_fc_w, L1_xattn_fc_b, L1_xattn_proj_w, L1_xattn_proj_b):
    import jax
    import jax.numpy as jnp

    def _L0_xattn_ref(hidden_states, audio_kv, audio_attention_mask, Wq, Wk, Wv, Wo, ln_gamma, ln_beta, gate):
        import jax, jax.numpy as jnp
        import numpy as np
        HIDDEN = 256
        HEADS = 16
        HEAD_DIM = HIDDEN // HEADS
        LN_EPS = 1e-05
        GATE_INIT = 0.5

        def _layer_norm(x, gamma, beta):
            mu = jnp.mean(x, axis=-1, keepdims=True)
            var = jnp.mean(jnp.square(x - mu), axis=-1, keepdims=True)
            return (x - mu) * jax.lax.rsqrt(var + LN_EPS) * gamma + beta
        B, Tt, D = hidden_states.shape
        Ta = audio_kv.shape[1]
        scale = HEAD_DIM ** (-0.5)
        a = _layer_norm(audio_kv, ln_gamma, ln_beta)
        Q = (hidden_states @ Wq.T).reshape(B, Tt, HEADS, HEAD_DIM).transpose(0, 2, 1, 3)
        K = (a @ Wk.T).reshape(B, Ta, HEADS, HEAD_DIM).transpose(0, 2, 1, 3)
        V = (a @ Wv.T).reshape(B, Ta, HEADS, HEAD_DIM).transpose(0, 2, 1, 3)
        scores = jnp.einsum('bhtd,bhsd->bhts', Q, K) * scale
        mask = audio_attention_mask[:, None, None, :]
        scores = jnp.where(mask, scores, jnp.float32(-jnp.inf))
        attn = jax.nn.softmax(scores, axis=-1)
        out = jnp.einsum('bhts,bhsd->bhtd', attn, V)
        out = out.transpose(0, 2, 1, 3).reshape(B, Tt, D)
        out = out @ Wo.T
        return hidden_states + jnp.tanh(gate) * out

    def _L1_xattn_ref(hidden_states, encoder_hidden_states, encoder_attention_mask, ln1_w, ln1_b, q_w, q_b, k_w, k_b, v_w, v_b, cproj_w, cproj_b, ln2_w, ln2_b, fc_w, fc_b, proj_w, proj_b):
        import jax, jax.numpy as jnp
        import numpy as np
        D = 256
        H = 16
        HD = D // H
        INNER = 4 * D
        EPS = 1e-05

        def layer_norm(x, w, b):
            mu = jnp.mean(x, axis=-1, keepdims=True)
            var = jnp.mean(jnp.square(x - mu), axis=-1, keepdims=True)
            return (x - mu) * jax.lax.rsqrt(var + EPS) * w + b
        B, LQ, _ = hidden_states.shape
        LK = encoder_hidden_states.shape[1]
        residual = hidden_states
        x = layer_norm(hidden_states, ln1_w, ln1_b)
        q = (x @ q_w + q_b).reshape(B, LQ, H, HD).transpose(0, 2, 1, 3)
        k = (encoder_hidden_states @ k_w + k_b).reshape(B, LK, H, HD).transpose(0, 2, 1, 3)
        v = (encoder_hidden_states @ v_w + v_b).reshape(B, LK, H, HD).transpose(0, 2, 1, 3)
        scale = 1.0 / np.sqrt(HD).astype(np.float32)
        scores = jnp.einsum('bhqd,bhkd->bhqk', q, k) * scale
        mask = encoder_attention_mask[:, None, None, :]
        mask_value = jnp.finfo(scores.dtype).min
        scores = jnp.where(mask, scores, mask_value)
        attn = jax.nn.softmax(scores, axis=-1)
        out = jnp.einsum('bhqk,bhkd->bhqd', attn, v)
        out = out.transpose(0, 2, 1, 3).reshape(B, LQ, D)
        out = out @ cproj_w + cproj_b
        hidden = out + residual
        residual = hidden
        y = layer_norm(hidden, ln2_w, ln2_b)
        y = jax.nn.gelu(y @ fc_w + fc_b, approximate=True)
        y = y @ proj_w + proj_b
        return residual + y
    x = _L0_xattn_ref(x, ctx_2048, mask_BxS2_bf1, L0_xattn_Wq, L0_xattn_Wk, L0_xattn_Wv, L0_xattn_Wo, L0_xattn_ln_gamma, L0_xattn_ln_beta, L0_xattn_gate)
    x = _L1_xattn_ref(x, ctx_2048, mask_BxS2_bf1, L1_xattn_ln1_w, L1_xattn_ln1_b, L1_xattn_q_w, L1_xattn_q_b, L1_xattn_k_w, L1_xattn_k_b, L1_xattn_v_w, L1_xattn_v_b, L1_xattn_cproj_w, L1_xattn_cproj_b, L1_xattn_ln2_w, L1_xattn_ln2_b, L1_xattn_fc_w, L1_xattn_fc_b, L1_xattn_proj_w, L1_xattn_proj_b)
    return x

_drawn_inputs = setup_inputs


def setup_inputs(seed=0):
    import zlib

    import numpy as np

    out = dict(_drawn_inputs(seed))
    spreads = {'L0_xattn_ln_gamma': (1.0, 0.6),
     'L0_xattn_ln_beta': (0.0, 0.8),
     'L1_xattn_ln1_w': (1.0, 0.6),
     'L1_xattn_ln1_b': (0.0, 0.8),
     'L1_xattn_q_b': (0.0, 0.8),
     'L1_xattn_k_b': (0.0, 0.8),
     'L1_xattn_v_b': (0.0, 0.267),
     'L1_xattn_cproj_b': (0.0, 0.1),
     'L1_xattn_ln2_w': (1.0, 0.6),
     'L1_xattn_ln2_b': (0.0, 0.8),
     'L1_xattn_fc_b': (0.0, 0.1),
     'L1_xattn_proj_b': (0.0, 0.1)}
    factors = {'L0_xattn_Wq': 8.0, 'L0_xattn_Wk': 8.0, 'L1_xattn_q_w': 8.0, 'L1_xattn_k_w': 8.0}
    for name, (base, spread) in spreads.items():
        noise = np.random.default_rng([zlib.crc32(name.encode()), seed]).standard_normal(out[name].shape)
        drawn = base * np.exp(spread * noise) if base else spread * noise
        out[name] = jnp.asarray(drawn.astype(out[name].dtype))
    for name, factor in factors.items():
        out[name] = (out[name] * factor).astype(out[name].dtype)
    return out
```

```python
from contextlib import ExitStack

import concourse.bass as bass
from concourse import mybir

F32 = mybir.dt.float32
BF16 = mybir.dt.bfloat16
ALU = mybir.AluOpType
ACT = mybir.ActivationFunctionType
AX = mybir.AxisListType

P = 128
B, T, S, D, H, DH, FF = 8, 256, 1601, 256, 16, 16, 1024
NT = -(-S // P)
LAST = S - (NT - 1) * P
FULL = (NT - 1) * P
CH = D // P
TT = T // P
HG = 4
NG = H // HG
VW = DH + 1
FT = FF // P
PARTS = ((0, 0), (0, 1), (1, 0), (1, 1), (0, 2), (2, 0))
RP = len(PARTS) * DH
RA = RP + 1
RB = RA + 3
CW = 401
CS = 400
LN_EPS = 1e-5
MASKED = -3.0e38
GELU_A, GELU_B = 0.7978845608028654, 0.044715
UNITS = NG * NT
LOOPS = 6

CHUNKS_AT = [[0, 1], [2, 3], [4, 5], [6, 7], [8, 9], [10, 11], [12, 13], [14], [15], [], [], [], []]

MAXIMA_AT = {10: ("MX", 1), 23: ("MX", 2), 36: ("MX", 3), 49: ("MX", 4)}
PREP0_AT = {9: ("T", 0), 11: ("T", 1), 12: ("T", 2), 13: ("T", 3), 14: ("T", 4), 15: ("T", 5), 16: ("T", 6),
            17: ("K", 0, 0), 18: ("K", 0, 1), 19: ("K", 0, 2), 20: ("K", 0, 3), 21: ("XT",), 22: ("Q",),
            24: ("K", 1, 0), 26: ("K", 1, 1), 28: ("K", 1, 2), 30: ("K", 1, 3),
            32: ("V", 0), 34: ("V", 1), 37: ("V", 2), 39: ("V", 3), 41: ("V", 4), 43: ("V", 5), 45: ("V", 6)}
PREP1_AT = {4: ("T", 0), 5: ("T", 1), 6: ("T", 2), 8: ("T", 3), 11: ("T", 4), 13: ("T", 5), 15: ("T", 6),
            17: ("K", 0, 0), 18: ("K", 0, 1), 19: ("K", 0, 2), 20: ("K", 0, 3), 21: ("XT",), 22: ("Q",),
            24: ("K", 1, 0), 26: ("K", 1, 1), 28: ("K", 1, 2), 30: ("K", 1, 3),
            33: ("V", 0), 35: ("V", 1), 37: ("V", 2), 39: ("V", 3), 41: ("V", 4), 43: ("V", 5), 45: ("V", 6)}
POST0_AT = {2: ("WO", 0), 3: ("WO", 1)}
POST1_AT = {2: ("WO", 0), 3: ("WO", 1), 7: ("HT",), 9: ("FC", 0), 12: ("FC", 1), 14: ("FC", 2), 16: ("FC", 3),
            25: ("PJ", 0), 27: ("PJ", 1)}


class Block:

    def __init__(self, n0, i, prep, prep_b, post, post_b):
        self.n0, self.i, self.par = n0, i, n0 % 2
        self.n = n0 + 2 * i
        self.prep, self.prep_b, self.post, self.post_b = prep, prep_b, post, post_b
        self.attends = 0 <= n0 < 16
        at = {}
        if self.attends:
            at.update({u: m for u, m in MAXIMA_AT.items() if n0 < 15 or m[1] < NG})
        for more in ({None: {}, 0: PREP0_AT, 1: PREP1_AT}[prep], {None: {}, 0: POST0_AT, 1: POST1_AT}[post]):
            assert not set(at) & set(more)
            at.update(more)
        if n0 < 0:
            at[100] = ("MX", NG)
        self.pieces = [at[u] for u in sorted(at)]
        self.at = {u: at[u] for u in sorted(at)}
        self.misc0 = 0

    def misc(self, piece):
        return self.misc0 + self.pieces.index(piece)

    def group(self, g):
        return 4 * self.n + g

    def split(self, o):
        return 9 * (self.n + 1) + o

    def split_ever(self, o):
        return self.n0 >= 0 or o >= 2

    def split_buffer(self, o):
        return (9 * (self.n0 + 1) + o) % 2

    def split_uses(self, o):
        return 9 * self.i + (9 * (self.n0 + 1) + o) // 2

    def uses_through(self, o, buf):
        s = 9 * (self.n0 + 1) + o
        last = s if s % 2 == buf else s - 1
        return 9 * self.i + last // 2 + 1


ORDER = {-1: (0, 0, None, 0), 0: (0, 1, None, 0), 1: (1, 0, 0, 0), 2: (0, 2, 0, 1), 3: (1, 1, 1, 0),
         14: (1, 7, 0, 7), 15: (None, 0, 1, 6), 16: (None, 0, 1, 7)}


def make_block(n0, i):
    prep, pb, post, qb = ORDER[n0]
    at_zero = {n: Block(n, 0, *ORDER[n]) for n in ORDER}
    count = {n: len(b.pieces) for n, b in at_zero.items()}
    blk = Block(n0, i, prep, pb + i, post, qb + i)
    per_loop = count[2] + count[3]
    if n0 <= 3:
        blk.misc0 = sum(count[n] for n in range(-1, n0)) + per_loop * i
    else:
        blk.misc0 = sum(count[n] for n in range(-1, 2)) + per_loop * LOOPS + sum(count[n] for n in range(14, n0))
    return blk


def walk(engine, visit):
    for n0 in (-1, 0, 1):
        visit(make_block(n0, 0))
    with engine.Fori(0, LOOPS) as i:
        for n0 in (2, 3):
            visit(make_block(n0, i))
    for n0 in (14, 15, 16):
        visit(make_block(n0, 0))


def split_no(piece):
    return 4 if piece[0] == "Q" else piece[2] + 5 * piece[1]


def chunk_cols(c):
    return 4 * P if c < 3 else LAST


def tile_rows(j):
    return P if j < NT - 1 else LAST


def build(nc, x, ctx, mask, Wq0, Wk0, Wv0, Wo0, gamma0, beta0, gate, ln1_w, ln1_b, q_w, q_b, k_w, k_b, v_w, v_b,
          o_w, o_b, ln2_w, ln2_b, fc_w, fc_b, pj_w, pj_b, out):
    scr_k = nc.dram_tensor("scr_k", [CH, 3, P, S], BF16, kind="Internal").ap()
    scr_q = nc.dram_tensor("scr_q", [3, CH, P, T], BF16, kind="Internal").ap()
    scr_max = nc.dram_tensor("scr_max", [2, 3 * HG * TT, P], BF16, kind="Internal").ap()
    scr_mask = nc.dram_tensor("scr_mask", [B, S], BF16, kind="Internal").ap()
    scr_vb = nc.dram_tensor("scr_vb", [D], F32, kind="Internal").ap()
    scr_row = nc.dram_tensor("scr_row", [2, D], F32, kind="Internal").ap()

    es = ExitStack()
    with es:
        def sb(name, shape, dt=F32):
            return es.enter_context(nc.sbuf_tensor(name, shape, dt))

        def sem(name):
            return es.enter_context(nc.semaphore(name))

        wq = [sb(f"wq{l}", [P, CH, D]) for l in range(2)]
        wk = [sb(f"wk{l}", [P, CH, D]) for l in range(2)]
        wv = [sb(f"wv{l}", [P, CH, D]) for l in range(2)]
        wo = [sb(f"wo{l}", [P, NG, D]) for l in range(2)]
        wfc = sb("wfc", [P, CH, FF])
        wpj = sb("wpj", [P, FT, D])
        pj_bias = sb("pj_bias", [P, D])
        ident = sb("ident", [P, P])
        ident_h = sb("ident_h", [P, P], BF16)
        cols = sb("cols", [P, 41])
        c_g0, c_b0, c_w1, c_b1, c_w2, c_b2 = (cols[:, 2 * k:2 * k + 2] for k in range(6))
        kbias = [cols[:, 12:14], cols[:, 14:16]]
        qbias = [cols[:, 16:18], cols[:, 18:20]]
        ln_eps_col = cols[:, 38:39]
        tgate, neg_half = cols[:, 20:21], cols[:, 21:22]
        fcbias = cols[:, 22:30]
        vb_pad = [cols[:, 30:34], cols[:, 34:38]]
        bias_row = sb("bias_row", [1, 2, D])

        ctxn = sb("ctxn", [P, NT, D])
        ctxt = sb("ctxt", [P, NT, CH, P])
        vals = [sb(f"vals{k}", [P, NT, H, VW]) for k in range(2)]
        parts = [sb(f"parts{k}", [P, 3, 4 * P], BF16) for k in range(2)]
        rest = sb("rest", [P, 2, 4 * P])
        kst = sb("kst", [RB, H, S], BF16)
        qst = sb("qst", [RB, H, T], BF16)
        prob = sb("prob", [P, 2, HG, T])
        maxes = sb("maxes", [P, 16])
        neg_max = sb("neg_max", [P, 8])
        max_parts = sb("max_parts", [P, 3, 8], BF16)
        max_rows = sb("max_rows", [3 * 8, P], BF16)
        o_raw = sb("o_raw", [P, T])
        o_den = sb("o_den", [P, T])
        o_t = sb("o_t", [P, NG, T])
        xin = [sb(f"xin{k}", [P, TT, D]) for k in range(2)]
        x1 = sb("x1", [P, TT, D])
        x1_kept = sb("x1_kept", [P, TT, D])
        normed = sb("normed", [P, TT, D])
        x_t = sb("x_t", [P, CH, T])
        hid = sb("hid", [P, TT, D])
        z = sb("z", [P, 2, T])
        z2 = sb("z2", [P, 2, T])
        g_t = sb("g_t", [P, FT, T])
        y = sb("y", [P, TT, D])
        st = sb("st", [P, NT, 6])
        mv = sb("mv", [P, NT, 2])
        rstd = sb("rstd", [P, NT])
        st2 = sb("st2", [P, TT, 6])
        mv2 = sb("mv2", [P, TT, 2])
        rstd2 = sb("rstd2", [P, TT])
        mask_u = g_t[0:B, 0:2, :].rearrange("b a c -> b (a c)").bitcast(mybir.dt.uint8)[:, 0:S]
        mask_h = g_t[0:B, 2:6, :].rearrange("b a c -> b (a c)").bitcast(BF16)[:, 0:S]

        p_sc = es.enter_context(nc.psum_tensor("p_sc", [P, 2, 512], F32))
        p_mx = es.enter_context(nc.psum_tensor("p_mx", [P, 2, 2, 512], F32))
        p_acc = es.enter_context(nc.psum_tensor("p_acc", [P, 512], F32))
        p_misc = es.enter_context(nc.psum_tensor("p_misc", [P, 512], F32))

        loaded = sem("loaded")
        raw_loaded = sem("raw_loaded")
        const_made = sem("const_made")
        w_turned = sem("w_turned")
        w_saved = sem("w_saved")
        bias_summed = sem("bias_summed")
        bias_saved = sem("bias_saved")
        folded = sem("folded")
        vb_moved = sem("vb_moved")
        row_summed = sem("row_summed")
        row_saved = sem("row_saved")
        rows_placed = sem("rows_placed")
        gate_ready = sem("gate_ready")
        mask_made = sem("mask_made")
        mask_stored = sem("mask_stored")
        pool_step = sem("pool_step")
        dve_step = sem("dve_step")
        scores_ready = sem("scores_ready")
        exp_done = sem("exp_done")
        chunk_ready = sem("chunk_ready")
        chunk_done = sem("chunk_done")
        weighed = sem("weighed")
        acc_saved = sem("acc_saved")
        den_step = sem("den_step")
        o_ready = sem("o_ready")
        max_step = sem("max_step")
        max_split = sem("max_split")
        max_out = sem("max_out")
        max_in = sem("max_in")
        misc_ready = sem("misc_ready")
        misc_saved = sem("misc_saved")
        high_ready = sem("high_ready")
        mid_ready = sem("mid_ready")
        low_ready = sem("low_ready")
        parts_out = [sem(f"parts_out{k}") for k in range(2)]
        k_in = [sem(f"k_in{m}") for m in range(CH)]
        q_in = [sem(f"q_in{m}") for m in range(CH)]
        ctx_in = sem("ctx_in")
        x_in = sem("x_in")
        ctx_stats = sem("ctx_stats")
        ctx_var = sem("ctx_var")
        ctx_eps = sem("ctx_eps")
        ctx_rstd = sem("ctx_rstd")
        ctx_normed = sem("ctx_normed")
        ln_stats = [sem(f"ln_stats{k}") for k in range(2)]
        ln_var = [sem(f"ln_var{k}") for k in range(2)]
        ln_eps = [sem(f"ln_eps{k}") for k in range(2)]
        ln_rstd = [sem(f"ln_rstd{k}") for k in range(2)]
        ln_done = [sem(f"ln_done{k}") for k in range(2)]
        kept = sem("kept")
        hid_biased = sem("hid_biased")
        square_ready = sem("square_ready")
        cube_ready = sem("cube_ready")
        tanh_ready = sem("tanh_ready")
        gelu_ready = sem("gelu_ready")
        y_out = sem("y_out")

        block = es.enter_context(nc.Block())

        raw = ctxt[:, :, :, :].rearrange("p a b c -> p (a b c)")
        raw_qkv = [raw[:, 512 * k:512 * k + 512].rearrange("p (c i) -> p c i", c=CH) for k in range(3)]
        raw_o = raw[:, 1536:2560].rearrange("p (c g q d) -> p c g q d", c=CH, g=NG, q=HG)
        N_RAW, N_LOAD = 3 + 2 * 16, 15 + 8 + 4
        LOADED, RAW_LOADED = 16 * N_LOAD, 16 * N_RAW

        def hold(engine, signal, value):
            if not isinstance(value, int):
                value = engine.to_reg(value)
            engine.wait_ge(const_made, 1)
            engine.wait_ge(signal, value)

        def attended_batch(blk):
            return {0: 0, 1: 1, 2: blk.i, 3: blk.i + 2, 14: 6, 15: 7}[blk.n0]

        def next_ctx(blk):
            if blk.n0 == 3:
                j = blk.i + 3
                return (j - j // B).with_bounds(min_val=2, max_val=B - 1)
            return {-1: 1, 0: 0, 1: 2, 2: blk.i + 1}[blk.n0]

        def ctx_load(sp, blk_b, after_misc):
            if after_misc is not None:
                hold(sp, misc_ready, after_misc)
            sp.dma_start(ctxn[:, 0:NT - 1, :], ctx[blk_b, 0:FULL, :].rearrange("(p j) d -> p j d", j=NT - 1)
                         ).then_inc(ctx_in, 16)
            sp.dma_start(ctxn[0:LAST, NT - 1, :], ctx[blk_b, FULL:S, :]).then_inc(ctx_in, 16)

        @block.sync
        def _(sp):
            with nc.allow_non_contiguous_dma(reason="feature vectors as columns, once"):
                for dst, src in ((c_g0, gamma0), (c_b0, beta0), (c_w1, ln1_w), (c_b1, ln1_b), (c_w2, ln2_w),
                                 (c_b2, ln2_b), (kbias[1], k_b), (qbias[1], q_b), (fcbias, fc_b)):
                    sp.dma_start(dst, src.rearrange("(c p) -> p c", p=P)).then_inc(loaded, 16)
            sp.wait_ge(const_made, 5)
            for k, w in enumerate((Wq0, Wk0, Wv0)):
                sp.dma_start(raw_qkv[k], w.rearrange("(c o) i -> o c i", o=P)).then_inc(raw_loaded, 16)
            for c in range(CH):
                for g in range(NG):
                    for q in range(HG):
                        h = HG * g + q
                        sp.dma_start(raw_o[:, c, g, q, 0:DH], Wo0[P * c:P * c + P, DH * h:DH * h + DH]
                                     ).then_inc(raw_loaded, 16)
            sp.wait_ge(const_made, 11)
            ctx_load(sp, 0, None)
            sp.dma_start(xin[0][:, :, :], x[0].rearrange("(p t) d -> p t d", t=TT)).then_inc(x_in, 16)
            sp.wait_ge(mask_made, 1)
            sp.dma_start(scr_mask, mask_h).then_inc(mask_stored, 16)
            sp.wait_ge(bias_saved, 3)
            with nc.allow_non_contiguous_dma(reason="a vector from columns, once"):
                sp.dma_start(scr_vb.rearrange("(c p) -> p c", p=P), cols[:, 39:41]).then_inc(vb_moved, 16)
                sp.wait_ge(vb_moved, 16)
                for q in range(HG):
                    sp.dma_start(vb_pad[0][32 * q:32 * q + DH, :],
                                 scr_vb.rearrange("(g q d) -> q d g", q=HG, d=DH)[q]).then_inc(vb_moved, 16)
            sp.wait_ge(row_saved, 2)
            for l in range(2):
                sp.dma_start(wo[l][DH:DH + 1, 0, :], bias_row[:, l, :]).then_inc(rows_placed, 16)
            sp.wait_ge(mask_stored, 16)

            def split_out(blk, piece):
                o = split_no(piece)
                buf = blk.split_buffer(o)
                first = blk.n0 < 0
                hold(sp, low_ready, blk.split(o) + 1)
                if piece[0] == "Q":
                    if not first:
                        for m in range(CH):
                            hold(sp, q_in[m], 96 * (blk.n + 1))
                    sp.dma_start(scr_q.rearrange("k m r t -> r k m t"),
                                 parts[buf][:, :, :].rearrange("r k (m t) -> r k m t", m=CH)
                                 ).then_inc(parts_out[buf], 16)
                else:
                    m, c = piece[1:]
                    if not first:
                        hold(sp, k_in[m], 112 * (blk.n + 1))
                    w = chunk_cols(c)
                    sp.dma_start(scr_k[m].rearrange("k r s -> r k s")[:, :, 512 * c:512 * c + w],
                                 parts[buf][:, :, 0:w]).then_inc(parts_out[buf], 16)

            def fetch_stacks(n, blk, m, blk_b, first):
                for buf in range(2):
                    hold(sp, parts_out[buf], 16 * blk.uses_through(4 if m == 0 else 8, buf))
                if not first:
                    hold(sp, scores_ready, 104 * (n - 1) + 52 * (m + 1))
                hs = slice(8 * m, 8 * m + 8)
                for j, (_, kp) in enumerate(PARTS):
                    sp.dma_start(kst[DH * j:DH * j + DH, hs, :], scr_k[m, kp].rearrange("(h d) s -> d h s", d=DH)
                                 ).then_inc(k_in[m], 16)
                sp.dma_start(kst[RP:RP + 1, hs, :], scr_mask[blk_b].unsqueeze(0).unsqueeze(0).broadcast_to([1, 8, S])
                             ).then_inc(k_in[m], 16)
                for j, (qp, _) in enumerate(PARTS):
                    sp.dma_start(qst[DH * j:DH * j + DH, hs, :], scr_q[qp, m].rearrange("(h d) t -> d h t", d=DH)
                                 ).then_inc(q_in[m], 16)

            def maxima_move(blk, g):
                G = blk.group(g)
                slot = g % 2
                hold(sp, misc_saved, blk.misc(("MX", g)) + 1)
                if blk.n0 > 0 or (blk.n0 == 0 and g >= 2):
                    hold(sp, max_in, 16 * (G - 1))
                sp.dma_start(scr_max[slot], max_rows[:, :]).then_inc(max_out, 16)
                hold(sp, max_out, 16 * (G + 1))
                heads = slice(HG * (g % NG), HG * (g % NG) + HG)
                sp.dma_start(qst[RA:RB, heads, :].rearrange("k h t -> k (h t)"),
                             scr_max[slot].rearrange("(k a) t -> k (a t)", k=3)).then_inc(max_in, 16)

            def visit(blk):
                n = blk.n
                if 0 <= blk.n0 < 16:
                    maker = Block(blk.n0 - 1, blk.i, None, 0, None, 0)
                    fetch_stacks(n, maker, 1, attended_batch(blk), blk.n0 == 0)
                if blk.n0 == 0:
                    sp.dma_start(xin[1][:, :, :], x[1].rearrange("(p t) d -> p t d", t=TT)).then_inc(x_in, 16)
                units = range(UNITS) if blk.attends else [u for u in blk.at]
                for u in units:
                    piece = blk.at.get(u)
                    kind = piece[0] if piece else None
                    if kind in ("K", "Q"):
                        split_out(blk, piece)
                    if piece == ("T", NT // 2) and blk.n0 < 14:
                        ctx_load(sp, next_ctx(blk), blk.misc(piece) + 1)
                    if piece == ("WO", 1) and blk.post == 0 and blk.prep == 0:
                        hold(sp, misc_saved, blk.misc(piece) + 1)
                        sp.dma_start(xin[1][:, :, :], x[blk.prep_b].rearrange("(p t) d -> p t d", t=TT)
                                     ).then_inc(x_in, 16)
                    if kind == "MX":
                        if blk.post == 1 and piece[1] == (NG if blk.n0 < 15 else NG - 1):
                            hold(sp, y_out, 16 * (blk.post_b + 1))
                        maxima_move(blk, piece[1])
                    if piece == ("PJ", 1):
                        hold(sp, misc_saved, blk.misc(piece) + 1)
                        sp.dma_start(out[blk.post_b].rearrange("(p t) d -> p t d", t=TT), y[:, :, :]
                                     ).then_inc(y_out, 16)
                    if blk.prep is not None and (u == 27 if blk.attends else piece == ("Q",)):
                        fetch_stacks(n + 1, blk, 0, blk.prep_b, blk.n0 < 0)

            walk(sp, visit)
            sp.wait_ge(y_out, 16 * B)

        def kept_at(blk, prep):
            return xin[0] if blk.n0 == (14 if prep == 1 else 16) else x1_kept

        @block.gpsimd
        def _(pool):
            pool.memset(ident[:, :], 0.0).then_inc(pool_step, 1)
            pool.memset(ident_h[:, :], 0.0).then_inc(pool_step, 1)
            pool.wait_ge(pool_step, 2)
            for t in (ident, ident_h):
                pool.affine_select(out=t[:, :], in_=t[:, :], compare_op=ALU.not_equal, fill=1.0, base=0,
                                   pattern=[[-1, P]], channel_multiplier=1).then_inc(const_made, 1)
            pool.memset(raw[:, 1536:2560], 0.0).then_inc(const_made, 1)
            for l in range(2):
                pool.memset(wo[l][:, :, :], 0.0).then_inc(const_made, 1)
            pool.memset(ln_eps_col, LN_EPS).then_inc(pool_step, 1)
            pool.memset(neg_half, -0.5).then_inc(const_made, 1)
            pool.memset(vb_pad[0], 0.0).then_inc(const_made, 1)
            pool.memset(vb_pad[1], 0.0).then_inc(const_made, 1)
            for k in range(2):
                pool.memset(vals[k][:, :, :, DH], 1.0).then_inc(const_made, 1)
            pool.memset(ctxn[:, NT - 1, :], 0.0).then_inc(const_made, 1)

            pool.wait_ge(pool_step, 3)
            pool.wait_ge(const_made, 11)

            def split_low(blk, piece):
                o = split_no(piece)
                s, buf = blk.split(o), blk.split_buffer(o)
                w = chunk_cols(piece[2]) if piece[0] == "K" else 512
                pool.wait_ge(mid_ready, s + 1)
                pool.tensor_tensor(parts[buf][:, 2, 0:w], rest[:, buf, 0:w], parts[buf][:, 1, 0:w], ALU.subtract
                                   ).then_inc(low_ready, 1)

            def inverse_root(var, dst, b, var_sem, eps_sem, out_sem):
                pool.wait_ge(var_sem, b + 1)
                pool.tensor_tensor(dst, var, ln_eps_col.broadcast_to(list(dst.shape)), ALU.add).then_inc(eps_sem, 1)
                pool.wait_ge(eps_sem, b + 1)
                pool.tensor_tensor(dst, dst, neg_half.broadcast_to(list(dst.shape)), ALU.pow).then_inc(out_sem, 1)

            def visit(blk):
                units = range(UNITS) if blk.attends else [-1] + [u for u in blk.at]
                for u in units:
                    piece = blk.at.get(u)
                    if blk.prep == 0 and u == (7 if blk.attends else -1):
                        inverse_root(mv[:, :, 1], rstd[:, :], blk.prep_b, ctx_var, ctx_eps, ctx_rstd)
                    if blk.prep == 1 and u == 5:
                        inverse_root(mv2[:, :, 1], rstd2[:, :], blk.prep_b, ln_var[0], ln_eps[0], ln_rstd[0])
                    if blk.prep == 1 and u == 7:
                        pool.tensor_copy(kept_at(blk, blk.prep)[:, :, :], x1[:, :, :]).then_inc(kept, 1)
                    if blk.post == 1 and piece == ("WO", 1):
                        inverse_root(mv2[:, :, 1], rstd2[:, :], blk.post_b, ln_var[1], ln_eps[1], ln_rstd[1])
                        pool.wait_ge(ln_done[1], blk.post_b + 1)
                        pool.tensor_tensor(hid[:, :, :], hid[:, :, :],
                                           pj_bias[:, :].unsqueeze(1).broadcast_to([P, TT, D]), ALU.add
                                           ).then_inc(hid_biased, 1)
                    if piece and piece[0] in ("K", "Q"):
                        split_low(blk, piece)

            walk(pool, visit)

        def follow(blk, k):
            at = {p: u for u, p in blk.at.items()}[("FC", k)]
            later = [u for u in (range(at + 1, UNITS) if blk.attends else blk.at) if u > at]
            return later[0]

        @block.scalar
        def _(act):
            for w, src in ((wq[1], q_w), (wk[1], k_w), (wv[1], v_w)):
                act.dma_start(w[:, :, :], src.rearrange("(c i) o -> i c o", i=P)).then_inc(loaded, 16)
            act.dma_start(wfc[:, :, :], fc_w.rearrange("(c i) o -> i c o", i=P)).then_inc(loaded, 16)
            act.dma_start(wpj[:, :, :], pj_w.rearrange("(f i) o -> i f o", i=P)).then_inc(loaded, 16)
            act.dma_start(mask_u, mask).then_inc(loaded, 16)
            act.wait_ge(const_made, 8)
            with nc.allow_non_contiguous_dma(reason="a bias spread over the heads' rows, once"):
                for q in range(HG):
                    act.dma_start(wo[1][32 * q:32 * q + DH, :, :],
                                  o_w.rearrange("(g q d) e -> q d g e", q=HG, d=DH)[q]).then_inc(loaded, 16)
                    act.dma_start(vb_pad[1][32 * q:32 * q + DH, :],
                                  v_b.rearrange("(g q d) -> q d g", q=HG, d=DH)[q]).then_inc(loaded, 16)
            act.dma_start(pj_bias[:, :], pj_b.unsqueeze(0).broadcast_to([P, D])).then_inc(loaded, 16)
            act.dma_start(tgate, gate.unsqueeze(0).broadcast_to([P, 1])).then_inc(loaded, 16)
            act.dma_start(y[0:1, 0, :], o_b.unsqueeze(0)).then_inc(loaded, 16)
            act.dma_start(y[0:1, 1, :], o_b.unsqueeze(0)).then_inc(loaded, 16)
            act.wait_ge(loaded, LOADED)
            act.activation(tgate, tgate, ACT.Tanh).then_inc(gate_ready, 1)

            def save_piece(blk, piece):
                kind, m = piece[0], blk.misc(piece)
                act.wait_ge(misc_ready, m + 1)
                if kind == "T":
                    k = piece[1]
                    if k < NT // 2:
                        act.activation(ctxt[:, 2 * k:2 * k + 2, :, :].rearrange("p j c s -> p (j c s)"),
                                       p_misc[:, :], ACT.Copy).then_inc(misc_saved, 1)
                    else:
                        act.activation(ctxt[:, NT - 1, :, 0:LAST],
                                       p_misc[:, 0:2 * P].rearrange("p (c s) -> p c s", c=CH)[:, :, 0:LAST],
                                       ACT.Copy).then_inc(misc_saved, 1)
                elif kind == "K":
                    o, w = split_no(piece), chunk_cols(piece[2])
                    buf = blk.split_buffer(o)
                    if blk.split_ever(o):
                        act.wait_ge(parts_out[buf], 16 * blk.split_uses(o))
                    act.activation(parts[buf][:, 0, 0:w], p_misc[:, 0:w], ACT.Identity,
                                   bias=kbias[blk.prep][:, piece[1]:piece[1] + 1]).then_inc(high_ready, 1)
                elif kind == "Q":
                    buf = blk.split_buffer(4)
                    act.wait_ge(parts_out[buf], 16 * blk.split_uses(4))
                    for c in range(CH):
                        ins = act.activation(parts[buf][:, 0, T * c:T * c + T], p_misc[:, T * c:T * c + T],
                                             ACT.Identity, bias=qbias[blk.prep][:, c:c + 1])
                    ins.then_inc(high_ready, 1)
                elif kind == "V":
                    k = piece[1]
                    dst = vals[1 - blk.par]
                    if k == 0 and blk.n0 >= 1:
                        act.wait_ge(weighed, UNITS * blk.n)
                    rows = tile_rows(2 * k)
                    js = slice(2 * k, min(2 * k + 2, NT))
                    nj = js.stop - js.start
                    act.activation(dst[0:rows, js, :, 0:DH],
                                   p_misc[0:rows, 0:D * nj].rearrange("p (j h d) -> p j h d", j=nj, h=H),
                                   ACT.Copy).then_inc(misc_saved, 1)
                elif kind in ("XT", "HT"):
                    act.activation(x_t[:, :, :].rearrange("p c t -> p (c t)"), p_misc[:, :], ACT.Copy
                                   ).then_inc(misc_saved, 1)
                elif kind == "FC":
                    k, b = piece[1], blk.post_b
                    if k:
                        act.wait_ge(gelu_ready, 4 * b + k)
                    for a in range(2):
                        f = 2 * k + a
                        ins = act.activation(z[:, a, :], p_misc[:, T * a:T * a + T], ACT.Identity,
                                             bias=fcbias[:, f:f + 1])
                    ins.then_inc(misc_saved, 1)
                    act.wait_ge(misc_saved, m + 1)
                    act.activation(z2[:, :, :], z[:, :, :], ACT.Square).then_inc(square_ready, 1)

            def tanh(blk, k):
                act.wait_ge(cube_ready, 4 * blk.post_b + k + 1)
                act.activation(z2[:, :, :], z2[:, :, :], ACT.Tanh, scale=GELU_A * GELU_B).then_inc(tanh_ready, 1)

            def exps(blk, u):
                j, rows = u % NT, tile_rows(u % NT)
                for half in range(2):
                    k = 104 * blk.n + 2 * u + half
                    act.wait_ge(scores_ready, k + 1)
                    if half == 0 and (blk.n0 > 0 or u >= 2):
                        act.wait_ge(weighed, UNITS * blk.n + u - 1)
                    act.activation(prob[0:rows, u % 2, 2 * half:2 * half + 2, :].rearrange("p h t -> p (h t)"),
                                   p_sc[0:rows, half, :], ACT.Exp).then_inc(exp_done, 1)

            def save_sums(G, through):
                act.wait_ge(weighed, through)
                if not isinstance(G, int) or G:
                    act.wait_ge(o_ready, G)
                act.activation(o_raw[:, :], p_acc[:, 0:T], ACT.Copy).then_inc(acc_saved, 1)

            def visit(blk):
                for u in (range(UNITS) if blk.attends else [0] + [u for u in blk.at]):
                    if blk.attends:
                        exps(blk, u)
                    if u % NT == 0 and (blk.attends and (blk.n0 > 0 or u) or (blk.n0 == 16 and u == 0)):
                        g = u // NT
                        save_sums(blk.group(g) - 1, UNITS * blk.n + u)
                    piece = blk.at.get(u)
                    if blk.post == 1:
                        for k in range(4):
                            if u == follow(blk, k):
                                tanh(blk, k)
                    if piece and piece[0] not in ("MX", "WO", "PJ"):
                        save_piece(blk, piece)

            for k, w in enumerate((wq[0], wk[0], wv[0])):
                act.wait_ge(w_turned, k + 1)
                act.activation(w[:, :, :].rearrange("p c o -> p (c o)"), p_sc[:, k % 2, :], ACT.Copy
                               ).then_inc(w_saved, 1)
            for k in range(2):
                act.wait_ge(w_turned, 4 + k)
                act.activation(wo[0][:, 2 * k:2 * k + 2, :].rearrange("p g e -> p (g e)"), p_mx[:, 0, k, :], ACT.Copy
                               ).then_inc(w_saved, 1)
            walk(act, visit)

        @block.vector
        def _(dve):
            dve.memset(p_acc[:, :], 0.0).then_inc(dve_step, 1)
            dve.memset(kst[RP:RB, :, :], 1.0).then_inc(dve_step, 1)
            dve.memset(qst[RP:RB, :, :], 1.0).then_inc(dve_step, 1)
            dve.wait_ge(loaded, LOADED)
            for src, dst in ((mask_u[:, 0:FULL].rearrange("b (p j) -> b j p", j=NT - 1),
                              mask_h[:, 0:FULL].rearrange("b (j p) -> b j p", j=NT - 1)),
                             (mask_u[:, FULL:S], mask_h[:, FULL:S])):
                ins = dve.tensor_scalar(dst, src, -1.0, -MASKED, ALU.add, ALU.mult)
            ins.then_inc(mask_made, 1)
            dve.wait_ge(bias_summed, 1)
            dve.tensor_copy(kbias[0], p_misc[:, 0:2]).then_inc(bias_saved, 1)
            dve.memset(qbias[0], 0.0).then_inc(bias_saved, 1)
            dve.tensor_copy(cols[:, 39:41], p_misc[:, 2:4]).then_inc(bias_saved, 1)
            dve.tensor_tensor(qbias[1], p_misc[:, 4:6], qbias[1], ALU.add).then_inc(bias_saved, 1)
            dve.tensor_tensor(fcbias, p_misc[:, 8:16], fcbias, ALU.add).then_inc(bias_saved, 1)
            dve.wait_ge(bias_saved, 5)
            scale = float(DH) ** -0.5
            dve.tensor_scalar(qbias[1], qbias[1], scale, None, ALU.mult).then_inc(folded, 1)
            for c in range(CH):
                dve.tensor_scalar(wk[0][:, c, :], wk[0][:, c, :], c_g0[:, c:c + 1], None, ALU.mult).then_inc(folded, 1)
                dve.tensor_scalar(wv[0][:, c, :], wv[0][:, c, :], c_g0[:, c:c + 1], None, ALU.mult).then_inc(folded, 1)
                dve.tensor_scalar(wq[0][:, c, :], wq[0][:, c, :], scale, None, ALU.mult).then_inc(folded, 1)
                dve.tensor_scalar(wq[1][:, c, :], wq[1][:, c, :], c_w1[:, c:c + 1], scale, ALU.mult, ALU.mult
                                  ).then_inc(folded, 1)
                dve.tensor_scalar(wfc[:, c, :], wfc[:, c, :], c_w2[:, c:c + 1], None, ALU.mult).then_inc(folded, 1)
            dve.wait_ge(row_summed, 1)
            dve.tensor_copy(bias_row[:, 0, :], p_misc[0:1, 0:D]).then_inc(row_saved, 1)
            dve.tensor_tensor(bias_row[:, 1, :], p_misc[0:1, D:2 * D], y[0:1, 0, :], ALU.add).then_inc(row_saved, 1)

            def reduce_chunk(blk, g, c):
                k = 16 * blk.group(g) + c
                dve.wait_ge(chunk_ready, k + 1)
                dve.tensor_reduce(maxes[:, c:c + 1], p_mx[:, c % 2, :, 0:CW], AX.XY, ALU.max).then_inc(chunk_done, 1)
                if c == 15:
                    split_maxima(blk.group(g))

            def split_maxima(G):
                dve.wait_ge(chunk_done, 16 * (G + 1))
                dve.tensor_reduce(neg_max[:, :], maxes[:, :].rearrange("p (a b) -> p a b", b=2), AX.X, ALU.max,
                                  negate=True).then_inc(max_step, 1)
                dve.wait_ge(max_step, 4 * G + 1)
                dve.tensor_copy(max_parts[:, 0, :], neg_max[:, :]).then_inc(max_step, 1)
                dve.wait_ge(max_step, 4 * G + 2)
                dve.tensor_tensor(neg_max[:, :], neg_max[:, :], max_parts[:, 0, :], ALU.subtract).then_inc(max_step, 1)
                dve.wait_ge(max_step, 4 * G + 3)
                dve.tensor_copy(max_parts[:, 1, :], neg_max[:, :]).then_inc(max_step, 1)
                dve.wait_ge(max_step, 4 * G + 4)
                dve.tensor_tensor(max_parts[:, 2, :], neg_max[:, :], max_parts[:, 1, :], ALU.subtract
                                  ).then_inc(max_split, 1)

            def divide(G, g):
                hold(dve, acc_saved, G + 1)
                dve.stream_shuffle(o_den[:, :], o_raw[:, :], [DH] * 32).then_inc(den_step, 1)
                dve.wait_ge(den_step, 2 * G + 1)
                dve.reciprocal(o_den[:, :], o_den[:, :]).then_inc(den_step, 1)
                dve.wait_ge(den_step, 2 * G + 2)
                dve.tensor_tensor(o_t[:, g, :], o_raw[:, :], o_den[:, :], ALU.mult).then_inc(o_ready, 1)

            def ctx_stat_tiles(blk, js):
                if js[0] == 0:
                    dve.wait_ge(ctx_in, 32 * (blk.n + 2))
                    if blk.n0 < 0:
                        dve.wait_ge(const_made, 11)
                for j in js:
                    ins = dve.bn_stats(st[:, j, :], ctxn[:, j, :])
                if js[-1] == NT - 1:
                    ins.then_inc(ctx_stats, 1)

            def ctx_var_all(blk):
                hold(dve, ctx_stats, blk.prep_b + 1)
                for j in range(NT):
                    ins = dve.bn_aggr(mv[:, j, :], st[:, j, :])
                ins.then_inc(ctx_var, 1)

            def ctx_apply(blk, js):
                if js[0] == 0:
                    dve.wait_ge(ctx_rstd, blk.prep_b + 1)
                for j in js:
                    dve.tensor_scalar(ctxn[:, j, :], ctxn[:, j, :], mv[:, j, 0:1], rstd[:, j:j + 1],
                                      ALU.subtract, ALU.mult).then_inc(ctx_normed, 1)

            def ln_rows(k, src, b):
                for t in range(TT):
                    ins = dve.bn_stats(st2[:, t, :], src[:, t, :])
                ins.then_inc(ln_stats[k], 1)
                hold(dve, ln_stats[k], b + 1)
                for t in range(TT):
                    ins = dve.bn_aggr(mv2[:, t, :], st2[:, t, :])
                ins.then_inc(ln_var[k], 1)

            def ln_apply(k, src, b):
                dve.wait_ge(ln_rstd[k], b + 1)
                for t in range(TT):
                    ins = dve.tensor_scalar(normed[:, t, :], src[:, t, :], mv2[:, t, 0:1], rstd2[:, t:t + 1],
                                            ALU.subtract, ALU.mult)
                ins.then_inc(ln_done[k], 1)

            def do_piece(blk, piece):
                kind, m = piece[0], blk.misc(piece)
                if kind == "MX":
                    dve.wait_ge(misc_ready, m + 1)
                    if blk.n0 >= 0:
                        dve.wait_ge(max_out, 16 * blk.group(piece[1]))
                    dve.tensor_copy(max_rows[:, :], p_misc[0:24, 0:P // 2].bitcast(BF16)).then_inc(misc_saved, 1)
                elif kind in ("K", "Q"):
                    o = split_no(piece)
                    s, buf = blk.split(o), blk.split_buffer(o)
                    bias = kbias[blk.prep][:, piece[1]:piece[1] + 1] if kind == "K" else None
                    w = chunk_cols(piece[2]) if kind == "K" else 512
                    dve.wait_ge(high_ready, s + 1)
                    if blk.split_ever(o):
                        dve.wait_ge(low_ready, s - 1)
                    if kind == "K":
                        dve.scalar_tensor_tensor(out=rest[:, buf, 0:w], in0=p_misc[:, 0:w], scalar=bias,
                                                 in1=parts[buf][:, 0, 0:w], op0=ALU.add, op1=ALU.subtract
                                                 ).then_inc(misc_saved, 1)
                    else:
                        for c in range(CH):
                            cs = slice(T * c, T * c + T)
                            ins = dve.scalar_tensor_tensor(out=rest[:, buf, cs], in0=p_misc[:, cs],
                                                           scalar=qbias[blk.prep][:, c:c + 1],
                                                           in1=parts[buf][:, 0, cs], op0=ALU.add, op1=ALU.subtract)
                        ins.then_inc(misc_saved, 1)
                    dve.wait_ge(misc_saved, m + 1)
                    dve.tensor_copy(parts[buf][:, 1, 0:w], rest[:, buf, 0:w]).then_inc(mid_ready, 1)
                elif kind == "WO":
                    t, b = piece[1], blk.post_b
                    dve.wait_ge(misc_ready, m + 1)
                    if blk.post == 0:
                        if t == 0 and blk.n0 != 1:
                            dve.wait_ge(kept, b)
                        if blk.n0 == 1:
                            dve.wait_ge(gate_ready, 1)
                        dve.scalar_tensor_tensor(out=x1[:, t, :], in0=p_misc[:, 0:D], scalar=tgate,
                                                 in1=xin[1 - blk.par][:, t, :], op0=ALU.mult, op1=ALU.add
                                                 ).then_inc(misc_saved, 1)
                    else:
                        if t == 0:
                            dve.wait_ge(kept, b + 1)
                        dve.tensor_tensor(hid[:, t, :], p_misc[:, 0:D], kept_at(blk, None)[:, t, :], ALU.add
                                          ).then_inc(misc_saved, 1)
                        if t == 1:
                            dve.wait_ge(misc_saved, m + 1)
                            ln_rows(1, hid, b)
                elif kind == "FC":
                    k, b = piece[1], blk.post_b
                    dve.wait_ge(square_ready, 4 * b + k + 1)
                    dve.scalar_tensor_tensor(out=z2[:, :, :], in0=z2[:, :, :], scalar=1.0 / GELU_B, in1=z[:, :, :],
                                             op0=ALU.add, op1=ALU.mult).then_inc(cube_ready, 1)
                elif kind == "PJ":
                    t, b = piece[1], blk.post_b
                    dve.wait_ge(misc_ready, m + 1)
                    if t == 0:
                        dve.wait_ge(hid_biased, b + 1)
                        if blk.n0 == 16:
                            dve.wait_ge(y_out, 16 * b)
                    dve.scalar_tensor_tensor(out=y[:, t, :], in0=p_misc[:, 0:D], scalar=0.5, in1=hid[:, t, :],
                                             op0=ALU.mult, op1=ALU.add).then_inc(misc_saved, 1)

            def gelu(blk, k):
                dve.wait_ge(tanh_ready, 4 * blk.post_b + k + 1)
                dve.scalar_tensor_tensor(out=g_t[:, 2 * k:2 * k + 2, :], in0=z2[:, :, :], scalar=1.0, in1=z[:, :, :],
                                         op0=ALU.add, op1=ALU.mult).then_inc(gelu_ready, 1)

            def visit(blk):
                if not blk.attends and blk.prep == 0:
                    ctx_stat_tiles(blk, range(NT))
                    ctx_var_all(blk)
                    ctx_apply(blk, range(NT))
                if blk.n0 == 16:
                    divide(blk.group(0) - 1, NG - 1)
                for u in (range(UNITS) if blk.attends else list(blk.at)):
                    piece = blk.at.get(u)
                    if blk.attends and (blk.n0 < 15 or u < 3 * NT):
                        for c in CHUNKS_AT[u % NT]:
                            reduce_chunk(blk, u // NT + 1, c)
                    if blk.n0 < 0 and piece and piece[0] == "MX":
                        for c in range(16):
                            reduce_chunk(blk, NG, c)
                    if blk.attends and u % NT == 0 and (blk.n0 > 0 or u):
                        divide(blk.group(u // NT) - 1, (u // NT - 1) % NG)
                    if blk.attends and blk.prep == 0:
                        if u <= 6:
                            ctx_stat_tiles(blk, range(2 * u, min(2 * u + 2, NT)))
                        if u == 6:
                            ctx_var_all(blk)
                        if 8 <= u <= 14:
                            ctx_apply(blk, range(2 * u - 16, min(2 * u - 14, NT)))
                    if blk.prep == 1 and u == 5:
                        if blk.post == 1:
                            dve.wait_ge(ln_done[1], blk.post_b + 1)
                        else:
                            dve.wait_ge(misc_saved, blk.misc(("WO", 1)) + 1)
                        ln_rows(0, x1, blk.prep_b)
                    if blk.post == 1 and (u == 4 if blk.attends else piece == ("HT",)):
                        ln_apply(1, hid, blk.post_b)
                    if blk.prep == 1 and u == 8:
                        if blk.post == 1:
                            dve.wait_ge(misc_saved, blk.misc(("HT",)) + 1)
                        ln_apply(0, x1, blk.prep_b)
                    if blk.post == 1:
                        for k in range(4):
                            if u == follow(blk, k):
                                gelu(blk, k)
                    if piece and piece[0] in ("MX", "K", "Q", "WO", "FC", "PJ"):
                        do_piece(blk, piece)

            walk(dve, visit)

        @block.tensor
        def _(pe):
            mm = nc.tensor.matmul
            pe.wait_ge(const_made, 10)
            pe.wait_ge(dve_step, 3)
            pe.wait_ge(raw_loaded, RAW_LOADED)
            for k in range(3):
                if k == 2:
                    pe.wait_ge(w_saved, 1)
                for ci in range(CH):
                    for co in range(CH):
                        ins = nc.tensor.transpose(p_sc[:, k % 2, D * ci + P * co:D * ci + P * co + P],
                                                  raw_qkv[k][:, co, P * ci:P * ci + P], ident[:, :])
                ins.then_inc(w_turned, 1)
            for k in range(2):
                for g in range(2):
                    for ce in range(CH):
                        ins = nc.tensor.transpose(
                            p_mx[:, 0, k, D * g + P * ce:D * g + P * ce + P],
                            raw_o[:, ce, 2 * k + g, :, :].rearrange("p q d -> p (q d)"), ident[:, :])
                ins.then_inc(w_turned, 1)
            pe.wait_ge(w_saved, 5)
            pe.wait_ge(loaded, LOADED)
            jobs = [(wk[0], c_b0, 0, CH), (wv[0], c_b0, 2, CH), (wq[1], c_b1, 4, CH), (wfc, c_b2, 8, FT)]
            for w, shift, col, nm in jobs:
                for m in range(nm):
                    for c in range(CH):
                        ins = mm(p_misc[:, col + m:col + m + 1], w[:, c, P * m:P * m + P], shift[:, c:c + 1],
                                 start=(c == 0), stop=(c == CH - 1))
            ins.then_inc(bias_summed, 1)
            pe.wait_ge(vb_moved, 16 * 5)
            pe.wait_ge(bias_saved, 5)
            for l in range(2):
                for g in range(NG):
                    ins = mm(p_misc[0:1, D * l:D * l + D], vb_pad[l][:, g:g + 1], wo[l][:, g, :],
                             start=(g == 0), stop=(g == NG - 1))
            ins.then_inc(row_summed, 1)
            pe.wait_ge(row_saved, 2)
            pe.wait_ge(folded, 1 + 5 * CH)

            def scores(blk, u):
                g, j = u // NT, u % NT
                rows = tile_rows(j)
                for half in range(2):
                    k = 104 * blk.n + 2 * u + half
                    if blk.n0 > 0 or u:
                        pe.wait_ge(exp_done, k - 1)
                    if half == 0 and j == 0:
                        pe.wait_ge(max_in, 16 * (blk.group(g) + 1))
                    for q in range(2):
                        h = HG * g + 2 * half + q
                        ins = mm(p_sc[0:rows, half, T * q:T * q + T], kst[0:RB, h, P * j:P * j + rows],
                                 qst[0:RB, h, :], start=True, stop=True)
                    ins.then_inc(scores_ready, 1)

            def chunk(blk, g, c):
                k = 16 * blk.group(g) + c
                if blk.n0 >= 0 or c >= 2:
                    pe.wait_ge(chunk_done, k - 1)
                at, gg = (blk.n + 1, 0) if g == NG else (blk.n, g)
                if c == 0 and gg % 2 == 0:
                    pe.wait_ge(k_in[gg // 2], 112 * (at + 1))
                    pe.wait_ge(q_in[gg // 2], 96 * (at + 1))
                h, t, half = HG * gg + c // 4, c // 2 % 2, c % 2
                for w in range(2):
                    s0 = 2 * CS * half + CS * w
                    ins = mm(p_mx[:, c % 2, w, 0:CW], qst[0:RA, h, P * t:P * t + P], kst[0:RA, h, s0:s0 + CW],
                             start=True, stop=True)
                ins.then_inc(chunk_ready, 1)

            def weigh(par, units_before, G, u, first):
                g, j = u // NT, u % NT
                rows = tile_rows(j)
                pe.wait_ge(exp_done, 2 * units_before + 2)
                if j == 0 and not first:
                    pe.wait_ge(acc_saved, G)
                for q in range(HG):
                    h = HG * g + q
                    ins = mm(p_acc[32 * q:32 * q + VW, 0:T],
                             vals[par][0:rows, j, h, :], prob[0:rows, u % 2, q, :],
                             start=(j == 0), stop=(j == NT - 1))
                ins.then_inc(weighed, 1)

            def do_piece(blk, piece):
                kind, m = piece[0], blk.misc(piece)
                if blk.n0 >= 0 or m:
                    pe.wait_ge(misc_saved, m)
                if kind == "T":
                    k = piece[1]
                    js = range(2 * k, min(2 * k + 2, NT))
                    if blk.prep == 0:
                        pe.wait_ge(ctx_normed, NT * blk.prep_b + js[-1] + 1)
                    elif k == 0:
                        pe.wait_ge(ctx_in, 32 * (blk.n + 2))
                    for j in js:
                        r = tile_rows(j)
                        for c in range(CH):
                            o = D * (j - js[0]) + P * c
                            ins = nc.tensor.transpose(p_misc[:, o:o + r], ctxn[0:r, j, P * c:P * c + P],
                                                      ident[0:r, 0:r])
                elif kind == "K":
                    mo, ck = piece[1:]
                    w = chunk_cols(ck)
                    for c in range(CH):
                        rhs = ctxt[:, 4 * ck:4 * ck + 4, c, :] if ck < 3 else ctxt[:, NT - 1, c, 0:LAST]
                        ins = mm(p_misc[:, 0:w], wk[blk.prep][:, c, P * mo:P * mo + P], rhs,
                                 start=(c == 0), stop=(c == CH - 1))
                elif kind == "V":
                    k = piece[1]
                    for j in range(2 * k, min(2 * k + 2, NT)):
                        r, o = tile_rows(j), D * (j % 2)
                        for c in range(CH):
                            ins = mm(p_misc[0:r, o:o + D], ctxt[:, j, c, 0:r], wv[blk.prep][:, c, :],
                                     start=(c == 0), stop=(c == CH - 1))
                elif kind in ("XT", "HT"):
                    if kind == "HT":
                        pe.wait_ge(ln_done[1], blk.post_b + 1)
                        src = normed
                    elif blk.prep == 1:
                        pe.wait_ge(ln_done[0], blk.prep_b + 1)
                        src = normed
                    else:
                        pe.wait_ge(x_in, 16 * (blk.prep_b + 1))
                        src = xin[1 - blk.par]
                    for c in range(CH):
                        for t in range(TT):
                            o = T * c + P * t
                            ins = nc.tensor.transpose(p_misc[:, o:o + P], src[:, t, P * c:P * c + P], ident[:, :])
                elif kind == "Q":
                    for mo in range(CH):
                        for c in range(CH):
                            ins = mm(p_misc[:, T * mo:T * mo + T], wq[blk.prep][:, c, P * mo:P * mo + P],
                                     x_t[:, c, :], start=(c == 0), stop=(c == CH - 1))
                elif kind == "WO":
                    t = piece[1]
                    pe.wait_ge(o_ready, blk.group(0))
                    pe.wait_ge(rows_placed, 32)
                    for g in range(NG):
                        ins = mm(p_misc[:, 0:D], o_t[:, g, P * t:P * t + P], wo[blk.post][:, g, :],
                                 start=(g == 0), stop=(g == NG - 1))
                elif kind == "FC":
                    for a in range(2):
                        f = 2 * piece[1] + a
                        for c in range(CH):
                            ins = mm(p_misc[:, T * a:T * a + T], wfc[:, c, P * f:P * f + P], x_t[:, c, :],
                                     start=(c == 0), stop=(c == CH - 1))
                elif kind == "PJ":
                    t = piece[1]
                    pe.wait_ge(gelu_ready, 4 * (blk.post_b + 1))
                    for f in range(FT):
                        ins = mm(p_misc[:, 0:D], g_t[:, f, P * t:P * t + P], wpj[:, f, :],
                                 start=(f == 0), stop=(f == FT - 1))
                elif kind == "MX":
                    pe.wait_ge(max_split, blk.group(piece[1]) + 1)
                    ins = nc.tensor.transpose(p_misc[0:24, 0:P // 2].bitcast(BF16),
                                              max_parts[:, :, :].rearrange("p k a -> p (k a)"), ident_h[:, :])
                ins.then_inc(misc_ready, 1)

            def weigh_last_of_before(blk):
                weigh(1 - blk.par, UNITS * blk.n - 1, 0, UNITS - 1, False)

            def visit(blk):
                for u in (range(UNITS) if blk.attends else list(blk.at)):
                    piece = blk.at.get(u)
                    cs = []
                    if blk.attends:
                        scores(blk, u)
                        if blk.n0 < 15 or u < 3 * NT:
                            cs = CHUNKS_AT[u % NT]
                        if cs:
                            chunk(blk, u // NT + 1, cs[0])
                        if u == 0:
                            if blk.n0 > 0:
                                weigh_last_of_before(blk)
                        else:
                            weigh(blk.par, UNITS * blk.n + u - 1, blk.group((u - 1) // NT), u - 1,
                                  blk.n0 == 0 and u == 1)
                        if len(cs) > 1:
                            chunk(blk, u // NT + 1, cs[1])
                    elif blk.n0 == 16 and u == list(blk.at)[0]:
                        weigh_last_of_before(blk)
                    if blk.n0 < 0 and piece[0] == "MX":
                        for c in range(16):
                            chunk(blk, NG, c)
                    if piece:
                        do_piece(blk, piece)

            walk(pe, visit)


_INS = ['x', 'ctx_2048', 'mask_BxS2_bf1', 'L0_xattn_Wq', 'L0_xattn_Wk', 'L0_xattn_Wv', 'L0_xattn_Wo',
        'L0_xattn_ln_gamma', 'L0_xattn_ln_beta', 'L0_xattn_gate', 'L1_xattn_ln1_w', 'L1_xattn_ln1_b', 'L1_xattn_q_w',
        'L1_xattn_q_b', 'L1_xattn_k_w', 'L1_xattn_k_b', 'L1_xattn_v_w', 'L1_xattn_v_b', 'L1_xattn_cproj_w',
        'L1_xattn_cproj_b', 'L1_xattn_ln2_w', 'L1_xattn_ln2_b', 'L1_xattn_fc_w', 'L1_xattn_fc_b', 'L1_xattn_proj_w',
        'L1_xattn_proj_b']


def kernel(**inputs):
    import numpy as _np
    import concourse.bacc as _bacc
    from concourse import mybir as _mybir
    from concourse.bass_utils import run_bass_kernel_spmd as _run

    nc = _bacc.Bacc("TRN2", target_bir_lowering=False, num_devices=1)
    arrays, args = {}, []
    for name in _INS:
        a = _np.ascontiguousarray(inputs[name])
        if a.dtype.kind == "b":
            a = a.view(_np.uint8)
        arrays[f"in_{name}_dram"] = a
        args.append(nc.dram_tensor(f"in_{name}_dram", a.shape, _mybir.dt.from_np(a.dtype), kind="ExternalInput").ap())
    args.append(nc.dram_tensor("out_0_dram", (B, T, D), F32, kind="ExternalOutput").ap())
    build(nc, *args)
    r = _run(nc, [arrays], core_ids=[0])
    return r.results[0]["out_0_dram"]
```

```python
from contextlib import ExitStack

import concourse.bass as bass
from concourse import mybir

F32 = mybir.dt.float32
BF16 = mybir.dt.bfloat16
ALU = mybir.AluOpType
ACT = mybir.ActivationFunctionType
AX = mybir.AxisListType

P = 128
B, T, S, D, H, DH, FF = 8, 256, 1601, 256, 16, 16, 1024
NT = -(-S // P)
LAST = S - (NT - 1) * P
FULL = (NT - 1) * P
CH = D // P
TT = T // P
HG = 4
NG = H // HG
VW = DH + 1
FT = FF // P
PARTS = ((0, 0), (0, 1), (1, 0), (1, 1), (0, 2), (2, 0))
RP = len(PARTS) * DH
RA = RP + 1
RB = RA + 3
CW = 401
CS = 400
LN_EPS = 1e-5
MASKED = -3.0e38
GELU_A, GELU_B = 0.7978845608028654, 0.044715
UNITS = NG * NT
LOOPS = 6

EARLY = 6
CHUNKS_AT = [[(1, 6)], [(1, 7)], [(1, 8)], [(1, 9), (1, 10)], [(1, 11)], [(1, 12), (1, 13)], [(1, 14)], [(1, 15)],
             [(2, 0)], [(2, 1)], [(2, 2)], [(2, 3)], [(2, 4), (2, 5)]]

MAXIMA_AT = {9: ("MX", 1), 22: ("MX", 2), 35: ("MX", 3), 48: ("MX", 4)}
VALUES_AT = {36: ("V", 0), 38: ("V", 1), 40: ("V", 2), 43: ("V", 3), 45: ("V", 4), 49: ("V", 5), 51: ("V", 6)}
PREP0_FIRST_AT = {10: ("T", 0), 11: ("T", 1), 12: ("T", 2), 13: ("T", 3), 14: ("T", 4), 15: ("T", 5), 16: ("T", 6),
                  17: ("K", 0, 0), 18: ("K", 0, 1), 19: ("K", 0, 2), 20: ("K", 0, 3), 21: ("XT",), 23: ("Q",),
                  25: ("K", 1, 0), 28: ("K", 1, 1), 30: ("K", 1, 2), 33: ("K", 1, 3)} | VALUES_AT
PREP0_AT = {3: ("T", 0), 6: ("T", 1), 8: ("T", 2), 10: ("T", 3), 11: ("T", 4), 13: ("T", 5), 14: ("T", 6),
            12: ("K", 0, 0), 15: ("K", 0, 1), 17: ("K", 0, 2), 19: ("K", 0, 3), 20: ("XT",), 21: ("Q",),
            24: ("K", 1, 0), 28: ("K", 1, 1), 30: ("K", 1, 2), 33: ("K", 1, 3)} | VALUES_AT
PREP1_AT = {1: ("T", 0), 2: ("T", 1), 3: ("T", 2), 4: ("T", 3), 6: ("T", 4), 8: ("T", 5), 11: ("T", 6),
            14: ("K", 0, 0), 16: ("K", 0, 1), 18: ("K", 0, 2), 19: ("XT",), 20: ("K", 0, 3), 23: ("Q",),
            25: ("K", 1, 0), 28: ("K", 1, 1), 30: ("K", 1, 2), 33: ("K", 1, 3)} | VALUES_AT
POST0_AT = {5: ("WO", 0), 7: ("WO", 1)}
POST1_AT = {5: ("WO", 0), 7: ("WO", 1), 10: ("HT",), 12: ("FC", 0), 17: ("FC", 1), 27: ("FC", 2), 32: ("FC", 3),
            37: ("PJ", 0), 41: ("PJ", 1)}
APPLY_AT = {0: 0, 4: 1, 6: 2, 7: 3, 8: 4, 10: 5, 11: 6}
STATS_AT = {31: 0, 32: 1, 34: 2, 36: 3, 37: 4, 42: 5, 43: 6}
CTX_LOAD_AT = (43, 22)
FETCHES = ((slice(0, 8), 2), (slice(8, 12), 3), (slice(12, 16), 4))


class Block:

    def __init__(self, n0, i, prep, prep_b, post, post_b):
        self.n0, self.i, self.par = n0, i, n0 % 2
        self.n = n0 + 2 * i
        self.prep, self.prep_b, self.post, self.post_b = prep, prep_b, post, post_b
        self.attends = 0 <= n0 < 16
        at = {}
        if self.attends:
            at.update({u: m for u, m in MAXIMA_AT.items() if n0 < 15 or m[1] < NG})
        for more in ({None: {}, 0: PREP0_AT if n0 == 2 else PREP0_FIRST_AT, 1: PREP1_AT}[prep], {None: {}, 0: POST0_AT, 1: POST1_AT}[post]):
            assert not set(at) & set(more)
            at.update(more)
        if n0 < 0:
            at[100] = ("MX", NG)
        self.pieces = [at[u] for u in sorted(at)]
        self.at = {u: at[u] for u in sorted(at)}
        self.misc0 = 0

    def misc(self, piece):
        return self.misc0 + self.pieces.index(piece)

    def group(self, g):
        return 4 * self.n + g

    def split(self, o):
        return 9 * (self.n + 1) + o

    def split_ever(self, o):
        return self.n0 >= 0 or o >= 2

    def split_buffer(self, o):
        return (9 * (self.n0 + 1) + o) % 2

    def split_uses(self, o):
        return 9 * self.i + (9 * (self.n0 + 1) + o) // 2

    def uses_through(self, o, buf):
        s = 9 * (self.n0 + 1) + o
        last = s if s % 2 == buf else s - 1
        return 9 * self.i + last // 2 + 1


ORDER = {-1: (0, 0, None, 0), 0: (0, 1, None, 0), 1: (1, 0, 0, 0), 2: (0, 2, 0, 1), 3: (1, 1, 1, 0),
         14: (1, 7, 0, 7), 15: (None, 0, 1, 6), 16: (None, 0, 1, 7)}


def make_block(n0, i):
    prep, pb, post, qb = ORDER[n0]
    at_zero = {n: Block(n, 0, *ORDER[n]) for n in ORDER}
    count = {n: len(b.pieces) for n, b in at_zero.items()}
    blk = Block(n0, i, prep, pb + i, post, qb + i)
    per_loop = count[2] + count[3]
    if n0 <= 3:
        blk.misc0 = sum(count[n] for n in range(-1, n0)) + per_loop * i
    else:
        blk.misc0 = sum(count[n] for n in range(-1, 2)) + per_loop * LOOPS + sum(count[n] for n in range(14, n0))
    return blk


def walk(engine, visit):
    for n0 in (-1, 0, 1):
        visit(make_block(n0, 0))
    with engine.Fori(0, LOOPS) as i:
        for n0 in (2, 3):
            visit(make_block(n0, i))
    for n0 in (14, 15, 16):
        visit(make_block(n0, 0))


def split_no(piece):
    return 4 if piece[0] == "Q" else piece[2] + 5 * piece[1]


def chunk_cols(c):
    return 4 * P if c < 3 else LAST


def unit_chunks(blk, u):
    if not blk.attends:
        return []
    through = NG + 2 if blk.n0 < 15 else NG
    return [(u // NT + ahead, c) for ahead, c in CHUNKS_AT[u % NT] if u // NT + ahead < through]


FIRST_CHUNKS = [(NG, c) for c in range(16)] + [(NG + 1, c) for c in range(EARLY)]


def tile_pair(k):
    return range(2 * k, min(2 * k + 2, NT))


def tile_rows(j):
    return P if j < NT - 1 else LAST


def build(nc, x, ctx, mask, Wq0, Wk0, Wv0, Wo0, gamma0, beta0, gate, ln1_w, ln1_b, q_w, q_b, k_w, k_b, v_w, v_b,
          o_w, o_b, ln2_w, ln2_b, fc_w, fc_b, pj_w, pj_b, out):
    scr_k = nc.dram_tensor("scr_k", [CH, 3, P, S], BF16, kind="Internal").ap()
    scr_q = nc.dram_tensor("scr_q", [3, CH, P, T], BF16, kind="Internal").ap()
    scr_max = nc.dram_tensor("scr_max", [2, 3 * HG * TT, P], BF16, kind="Internal").ap()
    scr_mask = nc.dram_tensor("scr_mask", [B, S], BF16, kind="Internal").ap()
    scr_vb = nc.dram_tensor("scr_vb", [D], F32, kind="Internal").ap()
    scr_row = nc.dram_tensor("scr_row", [2, D], F32, kind="Internal").ap()

    es = ExitStack()
    with es:
        def sb(name, shape, dt=F32):
            return es.enter_context(nc.sbuf_tensor(name, shape, dt))

        def sem(name):
            return es.enter_context(nc.semaphore(name))

        wq = [sb(f"wq{l}", [P, CH, D]) for l in range(2)]
        wk = [sb(f"wk{l}", [P, CH, D]) for l in range(2)]
        wv = [sb(f"wv{l}", [P, CH, D]) for l in range(2)]
        wo = [sb(f"wo{l}", [P, NG, D]) for l in range(2)]
        wfc = sb("wfc", [P, CH, FF])
        wpj = sb("wpj", [P, FT, D])
        pj_bias = sb("pj_bias", [P, D])
        ident = sb("ident", [P, P])
        ident_h = sb("ident_h", [P, P], BF16)
        cols = sb("cols", [P, 42])
        c_g0, c_b0, c_w1, c_b1, c_w2, c_b2 = (cols[:, 2 * k:2 * k + 2] for k in range(6))
        kbias = [cols[:, 12:14], cols[:, 14:16]]
        qbias = [cols[:, 16:18], cols[:, 18:20]]
        ln_eps_col, one_col = cols[:, 38:39], cols[:, 41:42]
        tgate, neg_half = cols[:, 20:21], cols[:, 21:22]
        fcbias = cols[:, 22:30]
        vb_pad = [cols[:, 30:34], cols[:, 34:38]]
        bias_row = sb("bias_row", [1, 2, D])

        ctxn = sb("ctxn", [P, NT, D])
        ctxt = sb("ctxt", [P, NT, CH, P])
        vals = [sb(f"vals{k}", [P, NT, H, VW]) for k in range(2)]
        parts = [sb(f"parts{k}", [P, 3, 4 * P], BF16) for k in range(2)]
        rest = sb("rest", [P, 2, 4 * P])
        kst = sb("kst", [RB, H, S], BF16)
        qst = sb("qst", [RB, H, T], BF16)
        prob = sb("prob", [P, 2, HG, T])
        maxes = sb("maxes", [P, 16])
        neg_max = sb("neg_max", [P, 8])
        max_parts = sb("max_parts", [P, 3, 8], BF16)
        max_rows = sb("max_rows", [3 * 8, P], BF16)
        o_raw = sb("o_raw", [P, T])
        o_den = sb("o_den", [P, T])
        o_t = sb("o_t", [P, NG, T])
        xin = [sb(f"xin{k}", [P, TT, D]) for k in range(2)]
        x1 = sb("x1", [P, TT, D])
        x1_kept = sb("x1_kept", [P, TT, D])
        normed = sb("normed", [P, TT, D])
        x_t = sb("x_t", [P, CH, T])
        hid = sb("hid", [P, TT, D])
        z = sb("z", [P, 2, T])
        z2 = sb("z2", [P, 2, T])
        g_t = sb("g_t", [P, FT, T])
        y = sb("y", [P, TT, D])
        st = sb("st", [P, NT, 6])
        mv = sb("mv", [P, NT, 2])
        rstd = sb("rstd", [P, NT])
        st2 = sb("st2", [P, TT, 6])
        mv2 = sb("mv2", [P, TT, 2])
        rstd2 = sb("rstd2", [P, TT])
        mask_u = g_t[0:B, 0:2, :].rearrange("b a c -> b (a c)").bitcast(mybir.dt.uint8)[:, 0:S]
        mask_h = g_t[0:B, 2:6, :].rearrange("b a c -> b (a c)").bitcast(BF16)[:, 0:S]

        p_sc = es.enter_context(nc.psum_tensor("p_sc", [P, 2, 512], F32))
        p_mx = es.enter_context(nc.psum_tensor("p_mx", [P, 2, 2, 512], F32))
        p_acc = es.enter_context(nc.psum_tensor("p_acc", [P, 512], F32))
        p_misc = es.enter_context(nc.psum_tensor("p_misc", [P, 512], F32))

        loaded = sem("loaded")
        raw_loaded = sem("raw_loaded")
        const_made = sem("const_made")
        w_turned = sem("w_turned")
        w_saved = sem("w_saved")
        bias_summed = sem("bias_summed")
        bias_saved = sem("bias_saved")
        folded = sem("folded")
        vb_moved = sem("vb_moved")
        row_summed = sem("row_summed")
        row_saved = sem("row_saved")
        rows_placed = sem("rows_placed")
        gate_ready = sem("gate_ready")
        mask_made = sem("mask_made")
        mask_stored = sem("mask_stored")
        pool_step = sem("pool_step")
        dve_step = sem("dve_step")
        scores_ready = sem("scores_ready")
        exp_done = sem("exp_done")
        chunk_ready = sem("chunk_ready")
        chunk_done = sem("chunk_done")
        weighed = sem("weighed")
        acc_saved = sem("acc_saved")
        den_step = sem("den_step")
        o_ready = sem("o_ready")
        max_step = sem("max_step")
        max_split = sem("max_split")
        max_out = sem("max_out")
        max_in = sem("max_in")
        misc_ready = sem("misc_ready")
        misc_saved = sem("misc_saved")
        high_ready = sem("high_ready")
        mid_ready = sem("mid_ready")
        low_ready = sem("low_ready")
        parts_out = [sem(f"parts_out{k}") for k in range(2)]
        k_in = [sem(f"k_in{k}") for k in range(3)]
        q_in = [sem(f"q_in{k}") for k in range(3)]
        ctx_in = sem("ctx_in")
        x_in = sem("x_in")
        ctx_stats = sem("ctx_stats")
        ctx_var = sem("ctx_var")
        ctx_eps = sem("ctx_eps")
        ctx_rstd = sem("ctx_rstd")
        ctx_normed = sem("ctx_normed")
        ln_stats = [sem(f"ln_stats{k}") for k in range(2)]
        ln_var = [sem(f"ln_var{k}") for k in range(2)]
        ln_eps = [sem(f"ln_eps{k}") for k in range(2)]
        ln_rstd = [sem(f"ln_rstd{k}") for k in range(2)]
        ln_done = [sem(f"ln_done{k}") for k in range(2)]
        kept = sem("kept")
        hid_biased = sem("hid_biased")
        square_done = sem("square_done")
        square_ready = sem("square_ready")
        cube_ready = sem("cube_ready")
        tanh_done = sem("tanh_done")
        tanh_ready = sem("tanh_ready")
        gelu_ready = sem("gelu_ready")
        y_out = sem("y_out")

        block = es.enter_context(nc.Block())

        raw = ctxt[:, :, :, :].rearrange("p a b c -> p (a b c)")
        raw_qkv = [raw[:, 512 * k:512 * k + 512].rearrange("p (c i) -> p c i", c=CH) for k in range(3)]
        raw_o = raw[:, 1536:2560].rearrange("p (c g q d) -> p c g q d", c=CH, g=NG, q=HG)
        N_RAW, N_LOAD = 3 + 2 * 16, 15 + 8 + 4
        LOADED, RAW_LOADED = 16 * N_LOAD, 16 * N_RAW

        def hold(engine, signal, value):
            if not isinstance(value, int):
                value = engine.to_reg(value)
            engine.wait_ge(const_made, 1)
            engine.wait_ge(signal, value)

        def attended_batch(blk):
            return {0: 0, 1: 1, 2: blk.i, 3: blk.i + 2, 14: 6, 15: 7}[blk.n0]

        def next_ctx(blk):
            if blk.n0 == 3:
                j = blk.i + 3
                return (j - j // B).with_bounds(min_val=2, max_val=B - 1)
            return {-1: 1, 0: 0, 1: 2, 2: blk.i + 1}[blk.n0]

        def next_prep_b(blk):
            return blk.i + (2 if blk.n0 == 1 else 3)

        def ctx_load(sp, blk_b, after_misc):
            if after_misc is not None:
                hold(sp, misc_ready, after_misc)
            sp.dma_start(ctxn[:, 0:NT - 1, :], ctx[blk_b, 0:FULL, :].rearrange("(p j) d -> p j d", j=NT - 1)
                         ).then_inc(ctx_in, 16)
            sp.dma_start(ctxn[0:LAST, NT - 1, :], ctx[blk_b, FULL:S, :]).then_inc(ctx_in, 16)

        @block.sync
        def _(sp):
            with nc.allow_non_contiguous_dma(reason="feature vectors as columns, once"):
                for dst, src in ((c_g0, gamma0), (c_b0, beta0), (c_w1, ln1_w), (c_b1, ln1_b), (c_w2, ln2_w),
                                 (c_b2, ln2_b), (kbias[1], k_b), (qbias[1], q_b), (fcbias, fc_b)):
                    sp.dma_start(dst, src.rearrange("(c p) -> p c", p=P)).then_inc(loaded, 16)
            sp.wait_ge(const_made, 5)
            for k, w in enumerate((Wq0, Wk0, Wv0)):
                sp.dma_start(raw_qkv[k], w.rearrange("(c o) i -> o c i", o=P)).then_inc(raw_loaded, 16)
            for c in range(CH):
                for g in range(NG):
                    for q in range(HG):
                        h = HG * g + q
                        sp.dma_start(raw_o[:, c, g, q, 0:DH], Wo0[P * c:P * c + P, DH * h:DH * h + DH]
                                     ).then_inc(raw_loaded, 16)
            sp.wait_ge(const_made, 11)
            ctx_load(sp, 0, None)
            sp.dma_start(xin[0][:, :, :], x[0].rearrange("(p t) d -> p t d", t=TT)).then_inc(x_in, 16)
            sp.wait_ge(mask_made, 1)
            sp.dma_start(scr_mask, mask_h).then_inc(mask_stored, 16)
            sp.wait_ge(bias_saved, 3)
            with nc.allow_non_contiguous_dma(reason="a vector from columns, once"):
                sp.dma_start(scr_vb.rearrange("(c p) -> p c", p=P), cols[:, 39:41]).then_inc(vb_moved, 16)
                sp.wait_ge(vb_moved, 16)
                for q in range(HG):
                    sp.dma_start(vb_pad[0][32 * q:32 * q + DH, :],
                                 scr_vb.rearrange("(g q d) -> q d g", q=HG, d=DH)[q]).then_inc(vb_moved, 16)
            sp.wait_ge(row_saved, 2)
            for l in range(2):
                sp.dma_start(wo[l][DH:DH + 1, 0, :], bias_row[:, l, :]).then_inc(rows_placed, 16)
            sp.wait_ge(mask_stored, 16)

            def split_out(blk, piece):
                o = split_no(piece)
                buf = blk.split_buffer(o)
                first = blk.n0 < 0
                hold(sp, low_ready, blk.split(o) + 1)
                if piece[0] == "Q":
                    if not first:
                        for k in range(3):
                            hold(sp, q_in[k], 96 * (blk.n + 1))
                    sp.dma_start(scr_q.rearrange("k m r t -> r k m t"),
                                 parts[buf][:, :, :].rearrange("r k (m t) -> r k m t", m=CH)
                                 ).then_inc(parts_out[buf], 16)
                else:
                    m, c = piece[1:]
                    if not first:
                        for k in ((0,), (1, 2))[m]:
                            hold(sp, k_in[k], 112 * (blk.n + 1))
                    w = chunk_cols(c)
                    sp.dma_start(scr_k[m].rearrange("k r s -> r k s")[:, :, 512 * c:512 * c + w],
                                 parts[buf][:, :, 0:w]).then_inc(parts_out[buf], 16)

            def fetch_stacks(n, blk, k, blk_b, first):
                hs, groups = FETCHES[k]
                for buf in range(2):
                    hold(sp, parts_out[buf], 16 * blk.uses_through(4 if k == 0 else 8, buf))
                if not first:
                    hold(sp, scores_ready, 104 * (n - 1) + 26 * groups)
                nh, m = hs.stop - hs.start, hs.start // 8
                rows = slice(DH * hs.start - P * m, DH * hs.stop - P * m)
                for j, (_, kp) in enumerate(PARTS):
                    sp.dma_start(kst[DH * j:DH * j + DH, hs, :], scr_k[m, kp, rows].rearrange("(h d) s -> d h s", d=DH)
                                 ).then_inc(k_in[k], 16)
                sp.dma_start(kst[RP:RP + 1, hs, :], scr_mask[blk_b].unsqueeze(0).unsqueeze(0).broadcast_to([1, nh, S])
                             ).then_inc(k_in[k], 16)
                for j, (qp, _) in enumerate(PARTS):
                    sp.dma_start(qst[DH * j:DH * j + DH, hs, :], scr_q[qp, m, rows].rearrange("(h d) t -> d h t", d=DH)
                                 ).then_inc(q_in[k], 16)

            def maxima_move(blk, g):
                G = blk.group(g)
                slot = g % 2
                hold(sp, misc_saved, blk.misc(("MX", g)) + 1)
                if blk.n0 > 0 or (blk.n0 == 0 and g >= 2):
                    hold(sp, max_in, 16 * (G - 1))
                sp.dma_start(scr_max[slot], max_rows[:, :]).then_inc(max_out, 16)
                hold(sp, max_out, 16 * (G + 1))
                heads = slice(HG * (g % NG), HG * (g % NG) + HG)
                sp.dma_start(qst[RA:RB, heads, :].rearrange("k h t -> k (h t)"),
                             scr_max[slot].rearrange("(k a) t -> k (a t)", k=3)).then_inc(max_in, 16)

            def visit(blk):
                n = blk.n
                if 0 <= blk.n0 < 16:
                    maker = Block(blk.n0 - 1, blk.i, None, 0, None, 0)
                    fetch_stacks(n, maker, 2, attended_batch(blk), blk.n0 == 0)
                if blk.n0 == 0:
                    sp.dma_start(xin[1][:, :, :], x[1].rearrange("(p t) d -> p t d", t=TT)).then_inc(x_in, 16)
                units = range(UNITS) if blk.attends else [u for u in blk.at]
                for u in units:
                    piece = blk.at.get(u)
                    kind = piece[0] if piece else None
                    if kind in ("K", "Q"):
                        split_out(blk, piece)
                    if piece == ("WO", 1) and blk.post == 0 and blk.prep == 0:
                        hold(sp, misc_saved, blk.misc(piece) + 1)
                        sp.dma_start(xin[1][:, :, :], x[blk.prep_b].rearrange("(p t) d -> p t d", t=TT)
                                     ).then_inc(x_in, 16)
                    if kind == "MX":
                        if blk.post == 1 and piece[1] == NG:
                            hold(sp, y_out, 16 * (blk.post_b + 1))
                        maxima_move(blk, piece[1])
                    if blk.n0 < 14 and (u == CTX_LOAD_AT[blk.par] if blk.attends else piece == ("T", NT // 2)):
                        ctx_load(sp, next_ctx(blk), blk.misc(("T", NT // 2)) + 1)
                    if piece == ("PJ", 1):
                        hold(sp, misc_saved, blk.misc(piece) + 1)
                        sp.dma_start(out[blk.post_b].rearrange("(p t) d -> p t d", t=TT), y[:, :, :]
                                     ).then_inc(y_out, 16)
                    if blk.prep is not None and (u == 26 if blk.attends else piece == ("Q",)):
                        fetch_stacks(n + 1, blk, 0, blk.prep_b, blk.n0 < 0)
                    if blk.prep is not None and (u == 40 if blk.attends else piece == ("K", 1, 3)):
                        fetch_stacks(n + 1, blk, 1, blk.prep_b, blk.n0 < 0)

            walk(sp, visit)
            sp.wait_ge(y_out, 16 * B)

        def kept_at(blk, prep):
            return xin[0] if blk.n0 == (14 if prep == 1 else 16) else x1_kept

        def gelu_steps(blk, u, after):
            units = list(range(UNITS)) if blk.attends else list(blk.at)
            back = units.index(u) - ((1, 2, 3, 4) if blk.attends else (0, 0, 1, 1))[after]
            piece = blk.at.get(units[back]) if back >= 0 and blk.post == 1 else None
            return [piece[1]] if piece and piece[0] == "FC" else []

        @block.gpsimd
        def _(pool):
            pool.memset(ident[:, :], 0.0).then_inc(pool_step, 1)
            pool.memset(ident_h[:, :], 0.0).then_inc(pool_step, 1)
            pool.memset(one_col, 1.0).then_inc(pool_step, 1)
            pool.wait_ge(pool_step, 3)
            for t in (ident, ident_h):
                pool.affine_select(out=t[:, :], in_=t[:, :], compare_op=ALU.not_equal, fill=1.0, base=0,
                                   pattern=[[-1, P]], channel_multiplier=1).then_inc(const_made, 1)
            pool.memset(raw[:, 1536:2560], 0.0).then_inc(const_made, 1)
            for l in range(2):
                pool.memset(wo[l][:, :, :], 0.0).then_inc(const_made, 1)
            pool.memset(ln_eps_col, LN_EPS).then_inc(pool_step, 1)
            pool.memset(neg_half, -0.5).then_inc(const_made, 1)
            pool.memset(vb_pad[0], 0.0).then_inc(const_made, 1)
            pool.memset(vb_pad[1], 0.0).then_inc(const_made, 1)
            for k in range(2):
                pool.memset(vals[k][:, :, :, DH], 1.0).then_inc(const_made, 1)
            pool.memset(ctxn[:, NT - 1, :], 0.0).then_inc(const_made, 1)

            pool.wait_ge(pool_step, 4)
            pool.wait_ge(const_made, 11)

            def split_low(blk, piece):
                o = split_no(piece)
                s, buf = blk.split(o), blk.split_buffer(o)
                w = chunk_cols(piece[2]) if piece[0] == "K" else 512
                pool.wait_ge(mid_ready, s + 1)
                pool.tensor_tensor(parts[buf][:, 2, 0:w], rest[:, buf, 0:w], parts[buf][:, 1, 0:w], ALU.subtract
                                   ).then_inc(low_ready, 1)

            def inverse_root(var, dst, b, var_sem, eps_sem, out_sem):
                pool.wait_ge(var_sem, b + 1)
                pool.tensor_tensor(dst, var, ln_eps_col.broadcast_to(list(dst.shape)), ALU.add).then_inc(eps_sem, 1)
                pool.wait_ge(eps_sem, b + 1)
                pool.tensor_tensor(dst, dst, neg_half.broadcast_to(list(dst.shape)), ALU.pow).then_inc(out_sem, 1)

            def ctx_apply(blk, js):
                if js[0] == 0:
                    hold(pool, ctx_rstd, blk.prep_b + 1)
                for j in js:
                    pool.tensor_scalar(ctxn[:, j, :], ctxn[:, j, :], mv[:, j, 0:1], rstd[:, j:j + 1],
                                       ALU.subtract, ALU.mult).then_inc(ctx_normed, 1)

            def cube(blk, k):
                hold(pool, square_ready, 4 * blk.post_b + k + 1)
                pool.tensor_tensor(z2[:, :, :], z2[:, :, :], z[:, :, :], ALU.mult).then_inc(cube_ready, 1)

            def gelu(blk, k):
                hold(pool, tanh_ready, 4 * blk.post_b + k + 1)
                pool.tensor_tensor(g_t[:, 2 * k:2 * k + 2, :], z2[:, :, :], z[:, :, :], ALU.mult).then_inc(gelu_ready, 1)

            def output(G, g):
                pool.wait_ge(den_step, 3 * G + 3)
                pool.tensor_tensor(o_t[:, g, :], o_raw[:, :], o_den[:, :], ALU.mult).then_inc(o_ready, 1)

            def visit(blk):
                units = range(UNITS) if blk.attends else [-1] + [u for u in blk.at]
                if blk.n0 == 16:
                    output(blk.group(0) - 1, NG - 1)
                for u in units:
                    piece = blk.at.get(u)
                    if blk.prep == 0 and blk.n0 < 2 and u == (7 if blk.attends else -1):
                        inverse_root(mv[:, :, 1], rstd[:, :], blk.prep_b, ctx_var, ctx_eps, ctx_rstd)
                    if blk.n0 in (1, 3) and u == max(STATS_AT) + 2:
                        inverse_root(mv[:, :, 1], rstd[:, :], next_prep_b(blk), ctx_var, ctx_eps, ctx_rstd)
                    if blk.prep == 1 and u == 10:
                        inverse_root(mv2[:, :, 1], rstd2[:, :], blk.prep_b, ln_var[0], ln_eps[0], ln_rstd[0])
                    if blk.prep == 1 and u == 11:
                        pool.tensor_copy(kept_at(blk, blk.prep)[:, :, :], x1[:, :, :]).then_inc(kept, 1)
                    if blk.post == 1 and piece == ("WO", 1):
                        inverse_root(mv2[:, :, 1], rstd2[:, :], blk.post_b, ln_var[1], ln_eps[1], ln_rstd[1])
                        pool.wait_ge(ln_done[1], blk.post_b + 1)
                        pool.tensor_tensor(hid[:, :, :], hid[:, :, :],
                                           pj_bias[:, :].unsqueeze(1).broadcast_to([P, TT, D]), ALU.add
                                           ).then_inc(hid_biased, 1)
                    if blk.n0 < 0 and u < 0:
                        ctx_apply(blk, range(NT))
                    if blk.n0 == 0 and 8 <= u <= 14:
                        ctx_apply(blk, tile_pair(u - 8))
                    if blk.n0 == 2 and u in APPLY_AT:
                        ctx_apply(blk, tile_pair(APPLY_AT[u]))
                    if u >= 0:
                        for k in gelu_steps(blk, u, 3):
                            gelu(blk, k)
                        for k in gelu_steps(blk, u, 1):
                            cube(blk, k)
                    if blk.attends and u % NT == 2 and (blk.n0 > 0 or u >= NT):
                        output(blk.group(u // NT) - 1, (u // NT - 1) % NG)
                    if piece and piece[0] in ("K", "Q"):
                        split_low(blk, piece)

            walk(pool, visit)

        @block.scalar
        def _(act):
            for w, src in ((wq[1], q_w), (wk[1], k_w), (wv[1], v_w)):
                act.dma_start(w[:, :, :], src.rearrange("(c i) o -> i c o", i=P)).then_inc(loaded, 16)
            act.dma_start(wfc[:, :, :], fc_w.rearrange("(c i) o -> i c o", i=P)).then_inc(loaded, 16)
            act.dma_start(wpj[:, :, :], pj_w.rearrange("(f i) o -> i f o", i=P)).then_inc(loaded, 16)
            act.dma_start(mask_u, mask).then_inc(loaded, 16)
            act.wait_ge(const_made, 8)
            with nc.allow_non_contiguous_dma(reason="a bias spread over the heads' rows, once"):
                for q in range(HG):
                    act.dma_start(wo[1][32 * q:32 * q + DH, :, :],
                                  o_w.rearrange("(g q d) e -> q d g e", q=HG, d=DH)[q]).then_inc(loaded, 16)
                    act.dma_start(vb_pad[1][32 * q:32 * q + DH, :],
                                  v_b.rearrange("(g q d) -> q d g", q=HG, d=DH)[q]).then_inc(loaded, 16)
            act.dma_start(pj_bias[:, :], pj_b.unsqueeze(0).broadcast_to([P, D])).then_inc(loaded, 16)
            act.dma_start(tgate, gate.unsqueeze(0).broadcast_to([P, 1])).then_inc(loaded, 16)
            act.dma_start(y[0:1, 0, :], o_b.unsqueeze(0)).then_inc(loaded, 16)
            act.dma_start(y[0:1, 1, :], o_b.unsqueeze(0)).then_inc(loaded, 16)
            act.wait_ge(loaded, LOADED)
            act.activation(tgate, tgate, ACT.Tanh).then_inc(gate_ready, 1)

            def save_piece(blk, piece):
                kind, m = piece[0], blk.misc(piece)
                act.wait_ge(misc_ready, m + 1)
                if kind == "T":
                    k = piece[1]
                    if k < NT // 2:
                        act.activation(ctxt[:, 2 * k:2 * k + 2, :, :].rearrange("p j c s -> p (j c s)"),
                                       p_misc[:, :], ACT.Copy).then_inc(misc_saved, 1)
                    else:
                        act.activation(ctxt[:, NT - 1, :, 0:LAST],
                                       p_misc[:, 0:2 * P].rearrange("p (c s) -> p c s", c=CH)[:, :, 0:LAST],
                                       ACT.Copy).then_inc(misc_saved, 1)
                elif kind == "K":
                    o, w = split_no(piece), chunk_cols(piece[2])
                    buf = blk.split_buffer(o)
                    if blk.split_ever(o):
                        act.wait_ge(parts_out[buf], 16 * blk.split_uses(o))
                    act.activation(parts[buf][:, 0, 0:w], p_misc[:, 0:w], ACT.Identity,
                                   bias=kbias[blk.prep][:, piece[1]:piece[1] + 1]).then_inc(high_ready, 1)
                elif kind == "Q":
                    buf = blk.split_buffer(4)
                    act.wait_ge(parts_out[buf], 16 * blk.split_uses(4))
                    for c in range(CH):
                        ins = act.activation(parts[buf][:, 0, T * c:T * c + T], p_misc[:, T * c:T * c + T],
                                             ACT.Identity, bias=qbias[blk.prep][:, c:c + 1])
                    ins.then_inc(high_ready, 1)
                elif kind == "V":
                    k = piece[1]
                    dst = vals[1 - blk.par]
                    if k == 0 and blk.n0 >= 1:
                        act.wait_ge(weighed, UNITS * blk.n)
                    rows = tile_rows(2 * k)
                    js = slice(2 * k, min(2 * k + 2, NT))
                    nj = js.stop - js.start
                    act.activation(dst[0:rows, js, :, 0:DH],
                                   p_misc[0:rows, 0:D * nj].rearrange("p (j h d) -> p j h d", j=nj, h=H),
                                   ACT.Copy).then_inc(misc_saved, 1)
                elif kind in ("XT", "HT"):
                    act.activation((y if kind == "XT" else x_t)[:, :, :].rearrange("p c t -> p (c t)"), p_misc[:, :],
                                   ACT.Copy).then_inc(misc_saved, 1)
                elif kind == "FC":
                    k, b = piece[1], blk.post_b
                    if k:
                        act.wait_ge(gelu_ready, 4 * b + k)
                    for a in range(2):
                        f = 2 * k + a
                        ins = act.activation(z[:, a, :], p_misc[:, T * a:T * a + T], ACT.Identity,
                                             bias=fcbias[:, f:f + 1])
                    ins.then_inc(misc_saved, 1)

            def square(blk, k):
                act.wait_ge(misc_saved, blk.misc(("FC", k)) + 1)
                act.activation(z2[:, :, :], z[:, :, :], ACT.Square).then_inc(square_done, 1)
                act.wait_ge(square_done, 4 * blk.post_b + k + 1)
                act.activation(z2[:, :, :], z2[:, :, :], ACT.Identity, bias=one_col, scale=GELU_B
                               ).then_inc(square_ready, 1)

            def tanh(blk, k):
                act.wait_ge(cube_ready, 4 * blk.post_b + k + 1)
                act.activation(z2[:, :, :], z2[:, :, :], ACT.Tanh, scale=GELU_A).then_inc(tanh_done, 1)
                act.wait_ge(tanh_done, 4 * blk.post_b + k + 1)
                act.activation(z2[:, :, :], z2[:, :, :], ACT.Identity, bias=one_col).then_inc(tanh_ready, 1)

            def exps(blk, u):
                j, rows = u % NT, tile_rows(u % NT)
                for half in range(2):
                    k = 104 * blk.n + 2 * u + half
                    act.wait_ge(scores_ready, k + 1)
                    if half == 0 and (blk.n0 > 0 or u >= 2):
                        act.wait_ge(weighed, UNITS * blk.n + u - 1)
                    act.activation(prob[0:rows, u % 2, 2 * half:2 * half + 2, :].rearrange("p h t -> p (h t)"),
                                   p_sc[0:rows, half, :], ACT.Exp).then_inc(exp_done, 1)

            def save_sums(G, through):
                act.wait_ge(weighed, through)
                if not isinstance(G, int) or G:
                    act.wait_ge(o_ready, G)
                act.activation(o_raw[:, :], p_acc[:, 0:T], ACT.Copy).then_inc(acc_saved, 1)

            def visit(blk):
                units = range(UNITS) if blk.attends else list(blk.at)
                for u in (units if blk.attends else [0, *units]):
                    if blk.attends:
                        exps(blk, u)
                    if u % NT == 0 and (blk.attends and (blk.n0 > 0 or u) or (blk.n0 == 16 and u == 0)):
                        g = u // NT
                        save_sums(blk.group(g) - 1, UNITS * blk.n + u)
                    piece = blk.at.get(u)
                    for k in gelu_steps(blk, u, 2) if u in units else []:
                        tanh(blk, k)
                    if blk.attends:
                        for k in gelu_steps(blk, u, 0):
                            square(blk, k)
                    if piece and piece[0] not in ("MX", "WO", "PJ"):
                        save_piece(blk, piece)
                    if not blk.attends and piece:
                        for k in gelu_steps(blk, u, 0):
                            square(blk, k)

            for k, w in enumerate((wq[0], wk[0], wv[0])):
                act.wait_ge(w_turned, k + 1)
                act.activation(w[:, :, :].rearrange("p c o -> p (c o)"), p_sc[:, k % 2, :], ACT.Copy
                               ).then_inc(w_saved, 1)
            for k in range(2):
                act.wait_ge(w_turned, 4 + k)
                act.activation(wo[0][:, 2 * k:2 * k + 2, :].rearrange("p g e -> p (g e)"), p_mx[:, 0, k, :], ACT.Copy
                               ).then_inc(w_saved, 1)
            walk(act, visit)

        @block.vector
        def _(dve):
            dve.memset(p_acc[:, :], 0.0).then_inc(dve_step, 1)
            dve.memset(kst[RP:RB, :, :], 1.0).then_inc(dve_step, 1)
            dve.memset(qst[RP:RB, :, :], 1.0).then_inc(dve_step, 1)
            dve.wait_ge(loaded, LOADED)
            for src, dst in ((mask_u[:, 0:FULL].rearrange("b (p j) -> b j p", j=NT - 1),
                              mask_h[:, 0:FULL].rearrange("b (j p) -> b j p", j=NT - 1)),
                             (mask_u[:, FULL:S], mask_h[:, FULL:S])):
                ins = dve.tensor_scalar(dst, src, -1.0, -MASKED, ALU.add, ALU.mult)
            ins.then_inc(mask_made, 1)
            dve.wait_ge(bias_summed, 1)
            dve.tensor_copy(kbias[0], p_misc[:, 0:2]).then_inc(bias_saved, 1)
            dve.memset(qbias[0], 0.0).then_inc(bias_saved, 1)
            dve.tensor_copy(cols[:, 39:41], p_misc[:, 2:4]).then_inc(bias_saved, 1)
            dve.tensor_tensor(qbias[1], p_misc[:, 4:6], qbias[1], ALU.add).then_inc(bias_saved, 1)
            dve.tensor_tensor(fcbias, p_misc[:, 8:16], fcbias, ALU.add).then_inc(bias_saved, 1)
            dve.wait_ge(bias_saved, 5)
            scale = float(DH) ** -0.5
            dve.tensor_scalar(qbias[1], qbias[1], scale, None, ALU.mult).then_inc(folded, 1)
            for c in range(CH):
                dve.tensor_scalar(wk[0][:, c, :], wk[0][:, c, :], c_g0[:, c:c + 1], None, ALU.mult).then_inc(folded, 1)
                dve.tensor_scalar(wv[0][:, c, :], wv[0][:, c, :], c_g0[:, c:c + 1], None, ALU.mult).then_inc(folded, 1)
                dve.tensor_scalar(wq[0][:, c, :], wq[0][:, c, :], scale, None, ALU.mult).then_inc(folded, 1)
                dve.tensor_scalar(wq[1][:, c, :], wq[1][:, c, :], c_w1[:, c:c + 1], scale, ALU.mult, ALU.mult
                                  ).then_inc(folded, 1)
                dve.tensor_scalar(wfc[:, c, :], wfc[:, c, :], c_w2[:, c:c + 1], None, ALU.mult).then_inc(folded, 1)
            dve.wait_ge(row_summed, 1)
            dve.tensor_copy(bias_row[:, 0, :], p_misc[0:1, 0:D]).then_inc(row_saved, 1)
            dve.tensor_tensor(bias_row[:, 1, :], p_misc[0:1, D:2 * D], y[0:1, 0, :], ALU.add).then_inc(row_saved, 1)

            def reduce_chunk(blk, g, c):
                k = 16 * blk.group(g) + c
                dve.wait_ge(chunk_ready, k + 1)
                dve.tensor_reduce(maxes[:, c:c + 1], p_mx[:, c % 2, :, 0:CW], AX.XY, ALU.max).then_inc(chunk_done, 1)
                if c == 15:
                    split_maxima(blk.group(g))

            def split_maxima(G):
                dve.wait_ge(chunk_done, 16 * (G + 1))
                dve.tensor_reduce(neg_max[:, :], maxes[:, :].rearrange("p (a b) -> p a b", b=2), AX.X, ALU.max,
                                  negate=True).then_inc(max_step, 1)
                dve.wait_ge(max_step, 4 * G + 1)
                dve.tensor_copy(max_parts[:, 0, :], neg_max[:, :]).then_inc(max_step, 1)
                dve.wait_ge(max_step, 4 * G + 2)
                dve.tensor_tensor(neg_max[:, :], neg_max[:, :], max_parts[:, 0, :], ALU.subtract).then_inc(max_step, 1)
                dve.wait_ge(max_step, 4 * G + 3)
                dve.tensor_copy(max_parts[:, 1, :], neg_max[:, :]).then_inc(max_step, 1)
                dve.wait_ge(max_step, 4 * G + 4)
                dve.tensor_tensor(max_parts[:, 2, :], neg_max[:, :], max_parts[:, 1, :], ALU.subtract
                                  ).then_inc(max_split, 1)

            def divide(G, g, step):
                if step == 0:
                    hold(dve, acc_saved, G + 1)
                    dve.stream_shuffle(o_den[:, :], o_raw[:, :], [DH] * 32).then_inc(den_step, 1)
                    return
                half = slice(P * (step - 1), P * step)
                dve.wait_ge(den_step, 3 * G + 1)
                dve.reciprocal(o_den[:, half], o_den[:, half]).then_inc(den_step, 1)

            def ctx_stat_tiles(blk, js, ahead):
                if js[0] == 0:
                    dve.wait_ge(ctx_in, 32 * (blk.n + 1 + ahead))
                    if blk.n0 < 0:
                        dve.wait_ge(const_made, 11)
                for j in js:
                    ins = dve.bn_stats(st[:, j, :], ctxn[:, j, :])
                if js[-1] == NT - 1:
                    ins.then_inc(ctx_stats, 1)

            def ctx_var_all(b):
                hold(dve, ctx_stats, b + 1)
                for j in range(NT):
                    ins = dve.bn_aggr(mv[:, j, :], st[:, j, :])
                ins.then_inc(ctx_var, 1)

            def ln_rows(k, src, b):
                for t in range(TT):
                    ins = dve.bn_stats(st2[:, t, :], src[:, t, :])
                ins.then_inc(ln_stats[k], 1)
                hold(dve, ln_stats[k], b + 1)
                for t in range(TT):
                    ins = dve.bn_aggr(mv2[:, t, :], st2[:, t, :])
                ins.then_inc(ln_var[k], 1)

            def ln_apply(k, src, b):
                dve.wait_ge(ln_rstd[k], b + 1)
                for t in range(TT):
                    ins = dve.tensor_scalar(normed[:, t, :], src[:, t, :], mv2[:, t, 0:1], rstd2[:, t:t + 1],
                                            ALU.subtract, ALU.mult)
                ins.then_inc(ln_done[k], 1)

            def do_piece(blk, piece):
                kind, m = piece[0], blk.misc(piece)
                if kind == "MX":
                    dve.wait_ge(misc_ready, m + 1)
                    if blk.n0 >= 0:
                        dve.wait_ge(max_out, 16 * blk.group(piece[1]))
                    dve.tensor_copy(max_rows[:, :], p_misc[0:24, 0:P // 2].bitcast(BF16)).then_inc(misc_saved, 1)
                elif kind in ("K", "Q"):
                    o = split_no(piece)
                    s, buf = blk.split(o), blk.split_buffer(o)
                    bias = kbias[blk.prep][:, piece[1]:piece[1] + 1] if kind == "K" else None
                    w = chunk_cols(piece[2]) if kind == "K" else 512
                    dve.wait_ge(high_ready, s + 1)
                    if blk.split_ever(o):
                        dve.wait_ge(low_ready, s - 1)
                    if kind == "K":
                        dve.scalar_tensor_tensor(out=rest[:, buf, 0:w], in0=p_misc[:, 0:w], scalar=bias,
                                                 in1=parts[buf][:, 0, 0:w], op0=ALU.add, op1=ALU.subtract
                                                 ).then_inc(misc_saved, 1)
                    else:
                        for c in range(CH):
                            cs = slice(T * c, T * c + T)
                            ins = dve.scalar_tensor_tensor(out=rest[:, buf, cs], in0=p_misc[:, cs],
                                                           scalar=qbias[blk.prep][:, c:c + 1],
                                                           in1=parts[buf][:, 0, cs], op0=ALU.add, op1=ALU.subtract)
                        ins.then_inc(misc_saved, 1)
                    dve.wait_ge(misc_saved, m + 1)
                    dve.tensor_copy(parts[buf][:, 1, 0:w], rest[:, buf, 0:w]).then_inc(mid_ready, 1)
                elif kind == "WO":
                    t, b = piece[1], blk.post_b
                    dve.wait_ge(misc_ready, m + 1)
                    if blk.post == 0:
                        if t == 0 and blk.n0 != 1:
                            dve.wait_ge(kept, b)
                        if blk.n0 == 1:
                            dve.wait_ge(gate_ready, 1)
                        dve.scalar_tensor_tensor(out=x1[:, t, :], in0=p_misc[:, 0:D], scalar=tgate,
                                                 in1=xin[1 - blk.par][:, t, :], op0=ALU.mult, op1=ALU.add
                                                 ).then_inc(misc_saved, 1)
                    else:
                        if t == 0:
                            dve.wait_ge(kept, b + 1)
                        dve.tensor_tensor(hid[:, t, :], p_misc[:, 0:D], kept_at(blk, None)[:, t, :], ALU.add
                                          ).then_inc(misc_saved, 1)
                        if t == 1:
                            dve.wait_ge(misc_saved, m + 1)
                            ln_rows(1, hid, b)
                elif kind == "PJ":
                    t, b = piece[1], blk.post_b
                    dve.wait_ge(misc_ready, m + 1)
                    if t == 0:
                        dve.wait_ge(hid_biased, b + 1)
                        if blk.n0 == 16:
                            dve.wait_ge(y_out, 16 * b)
                    dve.scalar_tensor_tensor(out=y[:, t, :], in0=p_misc[:, 0:D], scalar=0.5, in1=hid[:, t, :],
                                             op0=ALU.mult, op1=ALU.add).then_inc(misc_saved, 1)

            def visit(blk):
                if not blk.attends and blk.prep == 0:
                    ctx_stat_tiles(blk, range(NT), 1)
                    ctx_var_all(blk.prep_b)
                if blk.n0 == 16:
                    for step in range(3):
                        divide(blk.group(0) - 1, NG - 1, step)
                for u in (range(UNITS) if blk.attends else list(blk.at)):
                    piece = blk.at.get(u)
                    cs = unit_chunks(blk, u)
                    if blk.attends and piece and piece[0] == "MX":
                        do_piece(blk, piece)
                    if cs:
                        reduce_chunk(blk, *cs[0])
                    divides = blk.attends and (blk.n0 > 0 or u >= NT)
                    if divides and u % NT in (1, 2):
                        divide(blk.group(u // NT) - 1, (u // NT - 1) % NG, u % NT)
                    if blk.n0 < 0 and piece and piece[0] == "MX":
                        for g, c in FIRST_CHUNKS:
                            reduce_chunk(blk, g, c)
                    if blk.n0 == 0:
                        if u <= 6:
                            ctx_stat_tiles(blk, tile_pair(u), 1)
                        if u == 6:
                            ctx_var_all(blk.prep_b)
                    if blk.n0 in (1, 3) and u in STATS_AT:
                        ctx_stat_tiles(blk, tile_pair(STATS_AT[u]), 2)
                    if blk.n0 in (1, 3) and u == max(STATS_AT) + 1:
                        ctx_var_all(next_prep_b(blk))
                    if blk.post == 1 and (u == 8 if blk.attends else piece == ("HT",)):
                        ln_apply(1, hid, blk.post_b)
                    if blk.prep == 1 and u == 10:
                        if blk.post == 1:
                            dve.wait_ge(ln_done[1], blk.post_b + 1)
                        else:
                            dve.wait_ge(misc_saved, blk.misc(("WO", 1)) + 1)
                        ln_rows(0, x1, blk.prep_b)
                    if blk.prep == 1 and u == 13:
                        if blk.post == 1:
                            dve.wait_ge(misc_saved, blk.misc(("HT",)) + 1)
                        ln_apply(0, x1, blk.prep_b)
                    if piece and piece[0] in ("K", "Q", "WO", "PJ") or blk.n0 < 0 and piece[0] == "MX":
                        do_piece(blk, piece)
                    if len(cs) > 1:
                        reduce_chunk(blk, *cs[1])
                    if divides and u % NT == 0:
                        divide(blk.group(u // NT) - 1, (u // NT - 1) % NG, 0)

            walk(dve, visit)

        @block.tensor
        def _(pe):
            mm = nc.tensor.matmul
            pe.wait_ge(const_made, 10)
            pe.wait_ge(dve_step, 3)
            pe.wait_ge(raw_loaded, RAW_LOADED)
            for k in range(3):
                if k == 2:
                    pe.wait_ge(w_saved, 1)
                for ci in range(CH):
                    for co in range(CH):
                        ins = nc.tensor.transpose(p_sc[:, k % 2, D * ci + P * co:D * ci + P * co + P],
                                                  raw_qkv[k][:, co, P * ci:P * ci + P], ident[:, :])
                ins.then_inc(w_turned, 1)
            for k in range(2):
                for g in range(2):
                    for ce in range(CH):
                        ins = nc.tensor.transpose(
                            p_mx[:, 0, k, D * g + P * ce:D * g + P * ce + P],
                            raw_o[:, ce, 2 * k + g, :, :].rearrange("p q d -> p (q d)"), ident[:, :])
                ins.then_inc(w_turned, 1)
            pe.wait_ge(w_saved, 5)
            pe.wait_ge(loaded, LOADED)
            jobs = [(wk[0], c_b0, 0, CH), (wv[0], c_b0, 2, CH), (wq[1], c_b1, 4, CH), (wfc, c_b2, 8, FT)]
            for w, shift, col, nm in jobs:
                for m in range(nm):
                    for c in range(CH):
                        ins = mm(p_misc[:, col + m:col + m + 1], w[:, c, P * m:P * m + P], shift[:, c:c + 1],
                                 start=(c == 0), stop=(c == CH - 1))
            ins.then_inc(bias_summed, 1)
            pe.wait_ge(vb_moved, 16 * 5)
            pe.wait_ge(bias_saved, 5)
            for l in range(2):
                for g in range(NG):
                    ins = mm(p_misc[0:1, D * l:D * l + D], vb_pad[l][:, g:g + 1], wo[l][:, g, :],
                             start=(g == 0), stop=(g == NG - 1))
            ins.then_inc(row_summed, 1)
            pe.wait_ge(row_saved, 2)
            pe.wait_ge(folded, 1 + 5 * CH)

            def scores(blk, u):
                g, j = u // NT, u % NT
                rows = tile_rows(j)
                for half in range(2):
                    k = 104 * blk.n + 2 * u + half
                    if blk.n0 > 0 or u:
                        pe.wait_ge(exp_done, k - 1)
                    if half == 0 and j == 0:
                        pe.wait_ge(max_in, 16 * (blk.group(g) + 1))
                    for q in range(2):
                        h = HG * g + 2 * half + q
                        ins = mm(p_sc[0:rows, half, T * q:T * q + T], kst[0:RB, h, P * j:P * j + rows],
                                 qst[0:RB, h, :], start=True, stop=True)
                    ins.then_inc(scores_ready, 1)

            def chunk(blk, g, c):
                k = 16 * blk.group(g) + c
                if blk.n0 >= 0 or g > NG or c >= 2:
                    pe.wait_ge(chunk_done, k - 1)
                at, gg = (blk.n + 1, g - NG) if g >= NG else (blk.n, g)
                if c == 0 and gg != 1:
                    pe.wait_ge(k_in[max(gg - 1, 0)], 112 * (at + 1))
                    pe.wait_ge(q_in[max(gg - 1, 0)], 96 * (at + 1))
                h, t, half = HG * gg + c // 4, c // 2 % 2, c % 2
                for w in range(2):
                    s0 = 2 * CS * half + CS * w
                    ins = mm(p_mx[:, c % 2, w, 0:CW], qst[0:RA, h, P * t:P * t + P], kst[0:RA, h, s0:s0 + CW],
                             start=True, stop=True)
                ins.then_inc(chunk_ready, 1)

            def weigh(par, units_before, G, u, first):
                g, j = u // NT, u % NT
                rows = tile_rows(j)
                pe.wait_ge(exp_done, 2 * units_before + 2)
                if j == 0 and not first:
                    pe.wait_ge(acc_saved, G)
                for q in range(HG):
                    h = HG * g + q
                    ins = mm(p_acc[32 * q:32 * q + VW, 0:T],
                             vals[par][0:rows, j, h, :], prob[0:rows, u % 2, q, :],
                             start=(j == 0), stop=(j == NT - 1))
                ins.then_inc(weighed, 1)

            def do_piece(blk, piece):
                kind, m = piece[0], blk.misc(piece)
                if blk.n0 >= 0 or m:
                    pe.wait_ge(misc_saved, m)
                if kind == "T":
                    k = piece[1]
                    js = range(2 * k, min(2 * k + 2, NT))
                    if blk.prep == 0:
                        pe.wait_ge(ctx_normed, NT * blk.prep_b + js[-1] + 1)
                    elif k == 0:
                        pe.wait_ge(ctx_in, 32 * (blk.n + 2))
                    for j in js:
                        r = tile_rows(j)
                        for c in range(CH):
                            o = D * (j - js[0]) + P * c
                            ins = nc.tensor.transpose(p_misc[:, o:o + r], ctxn[0:r, j, P * c:P * c + P],
                                                      ident[0:r, 0:r])
                elif kind == "K":
                    mo, ck = piece[1:]
                    w = chunk_cols(ck)
                    for c in range(CH):
                        rhs = ctxt[:, 4 * ck:4 * ck + 4, c, :] if ck < 3 else ctxt[:, NT - 1, c, 0:LAST]
                        ins = mm(p_misc[:, 0:w], wk[blk.prep][:, c, P * mo:P * mo + P], rhs,
                                 start=(c == 0), stop=(c == CH - 1))
                elif kind == "V":
                    k = piece[1]
                    for j in range(2 * k, min(2 * k + 2, NT)):
                        r, o = tile_rows(j), D * (j % 2)
                        for c in range(CH):
                            ins = mm(p_misc[0:r, o:o + D], ctxt[:, j, c, 0:r], wv[blk.prep][:, c, :],
                                     start=(c == 0), stop=(c == CH - 1))
                elif kind in ("XT", "HT"):
                    if kind == "HT":
                        pe.wait_ge(ln_done[1], blk.post_b + 1)
                        src = normed
                    elif blk.prep == 1:
                        pe.wait_ge(ln_done[0], blk.prep_b + 1)
                        src = normed
                    else:
                        pe.wait_ge(x_in, 16 * (blk.prep_b + 1))
                        src = xin[1 - blk.par]
                    for c in range(CH):
                        for t in range(TT):
                            o = T * c + P * t
                            ins = nc.tensor.transpose(p_misc[:, o:o + P], src[:, t, P * c:P * c + P], ident[:, :])
                elif kind == "Q":
                    for mo in range(CH):
                        for c in range(CH):
                            ins = mm(p_misc[:, T * mo:T * mo + T], wq[blk.prep][:, c, P * mo:P * mo + P],
                                     y[:, c, :], start=(c == 0), stop=(c == CH - 1))
                elif kind == "WO":
                    t = piece[1]
                    pe.wait_ge(o_ready, blk.group(0))
                    pe.wait_ge(rows_placed, 32)
                    for g in range(NG):
                        ins = mm(p_misc[:, 0:D], o_t[:, g, P * t:P * t + P], wo[blk.post][:, g, :],
                                 start=(g == 0), stop=(g == NG - 1))
                elif kind == "FC":
                    for a in range(2):
                        f = 2 * piece[1] + a
                        for c in range(CH):
                            ins = mm(p_misc[:, T * a:T * a + T], wfc[:, c, P * f:P * f + P], x_t[:, c, :],
                                     start=(c == 0), stop=(c == CH - 1))
                elif kind == "PJ":
                    t = piece[1]
                    pe.wait_ge(gelu_ready, 4 * (blk.post_b + 1))
                    for f in range(FT):
                        ins = mm(p_misc[:, 0:D], g_t[:, f, P * t:P * t + P], wpj[:, f, :],
                                 start=(f == 0), stop=(f == FT - 1))
                elif kind == "MX":
                    pe.wait_ge(max_split, blk.group(piece[1]) + 1)
                    ins = nc.tensor.transpose(p_misc[0:24, 0:P // 2].bitcast(BF16),
                                              max_parts[:, :, :].rearrange("p k a -> p (k a)"), ident_h[:, :])
                ins.then_inc(misc_ready, 1)

            def weigh_last_of_before(blk):
                weigh(1 - blk.par, UNITS * blk.n - 1, 0, UNITS - 1, False)

            def visit(blk):
                for u in (range(UNITS) if blk.attends else list(blk.at)):
                    piece = blk.at.get(u)
                    cs = unit_chunks(blk, u)
                    if blk.attends:
                        scores(blk, u)
                        if piece and piece[0] == "MX":
                            do_piece(blk, piece)
                        if cs:
                            chunk(blk, *cs[0])
                        if piece and piece[0] != "MX":
                            do_piece(blk, piece)
                        if u == 0:
                            if blk.n0 > 0:
                                weigh_last_of_before(blk)
                        else:
                            weigh(blk.par, UNITS * blk.n + u - 1, blk.group((u - 1) // NT), u - 1,
                                  blk.n0 == 0 and u == 1)
                        if len(cs) > 1:
                            chunk(blk, *cs[1])
                    elif blk.n0 == 16 and u == list(blk.at)[0]:
                        weigh_last_of_before(blk)
                    if blk.n0 < 0 and piece[0] == "MX":
                        for g, c in FIRST_CHUNKS:
                            chunk(blk, g, c)
                    if piece and not blk.attends:
                        do_piece(blk, piece)

            walk(pe, visit)


_INS = ['x', 'ctx_2048', 'mask_BxS2_bf1', 'L0_xattn_Wq', 'L0_xattn_Wk', 'L0_xattn_Wv', 'L0_xattn_Wo',
        'L0_xattn_ln_gamma', 'L0_xattn_ln_beta', 'L0_xattn_gate', 'L1_xattn_ln1_w', 'L1_xattn_ln1_b', 'L1_xattn_q_w',
        'L1_xattn_q_b', 'L1_xattn_k_w', 'L1_xattn_k_b', 'L1_xattn_v_w', 'L1_xattn_v_b', 'L1_xattn_cproj_w',
        'L1_xattn_cproj_b', 'L1_xattn_ln2_w', 'L1_xattn_ln2_b', 'L1_xattn_fc_w', 'L1_xattn_fc_b', 'L1_xattn_proj_w',
        'L1_xattn_proj_b']


def kernel(**inputs):
    import numpy as _np
    import concourse.bacc as _bacc
    from concourse import mybir as _mybir
    from concourse.bass_utils import run_bass_kernel_spmd as _run

    nc = _bacc.Bacc("TRN2", target_bir_lowering=False, num_devices=1)
    arrays, args = {}, []
    for name in _INS:
        a = _np.ascontiguousarray(inputs[name])
        if a.dtype.kind == "b":
            a = a.view(_np.uint8)
        arrays[f"in_{name}_dram"] = a
        args.append(nc.dram_tensor(f"in_{name}_dram", a.shape, _mybir.dt.from_np(a.dtype), kind="ExternalInput").ap())
    args.append(nc.dram_tensor("out_0_dram", (B, T, D), F32, kind="ExternalOutput").ap())
    build(nc, *args)
    r = _run(nc, [arrays], core_ids=[0])
    return r.results[0]["out_0_dram"]
```

```python
from contextlib import ExitStack

import concourse.bass as bass
from concourse import mybir

F32 = mybir.dt.float32
BF16 = mybir.dt.bfloat16
ALU = mybir.AluOpType
ACT = mybir.ActivationFunctionType
AX = mybir.AxisListType

P = 128
B, T, S, D, H, DH, FF = 8, 256, 1601, 256, 16, 16, 1024
NT = -(-S // P)
LAST = S - (NT - 1) * P
FULL = (NT - 1) * P
CH = D // P
TT = T // P
HG = 4
NG = H // HG
VW = DH + 1
FT = FF // P
PARTS = ((0, 0), (0, 1), (1, 0), (1, 1), (0, 2), (2, 0))
RP = len(PARTS) * DH
RA = RP + 1
RB = RA + 3
CW = 401
CS = 400
LN_EPS = 1e-5
MASKED = -3.0e38
GELU_A, GELU_B = 0.7978845608028654, 0.044715
UNITS = NG * NT
LOOPS = 6

DOUBLES = ({6, 7, 12, 15, 17, 23, 28, 33, 39, 41, 45, 51},
           {5, 7, 12, 14, 19, 23, 25, 30, 37, 40, 44, 49})
EARLY = 6
for doubles in DOUBLES:
    assert all(sum(n - 5 <= u < n + 8 for u in doubles) == 3 for n in (13, 26, 39))
    assert sum(u < 8 for u in doubles) == 2 and sum(u >= 47 for u in doubles) == EARLY - 5

MAXIMA_AT = {9: ("MX", 1), 22: ("MX", 2), 35: ("MX", 3), 48: ("MX", 4)}
PREP0_FIRST_AT = {10: ("T", 0), 11: ("T", 1), 12: ("T", 2), 13: ("T", 3), 14: ("T", 4), 15: ("T", 5), 16: ("T", 6),
                  17: ("K", 0, 0), 18: ("K", 0, 1), 19: ("K", 0, 2), 20: ("K", 0, 3), 21: ("XT",), 23: ("Q",),
                  25: ("K", 1, 0), 28: ("K", 1, 1), 33: ("K", 1, 2), 36: ("K", 1, 3),
                  31: ("V", 0), 38: ("V", 1), 40: ("V", 2), 43: ("V", 3), 45: ("V", 4), 49: ("V", 5), 51: ("V", 6)}
PREP0_AT = {3: ("T", 0), 6: ("T", 1), 8: ("T", 2), 10: ("T", 3), 11: ("T", 4), 12: ("K", 0, 0), 14: ("T", 5),
            15: ("K", 0, 1), 16: ("T", 6), 17: ("K", 0, 2), 18: ("XT",), 20: ("K", 0, 3), 23: ("Q",),
            25: ("K", 1, 0), 27: ("K", 1, 1), 31: ("V", 0), 33: ("K", 1, 2), 36: ("K", 1, 3), 38: ("V", 1),
            40: ("V", 2), 43: ("V", 3), 45: ("V", 4), 49: ("V", 5), 51: ("V", 6)}
PREP1_AT = {1: ("T", 0), 2: ("T", 1), 3: ("T", 2), 4: ("T", 3), 6: ("T", 4), 8: ("T", 5), 11: ("T", 6),
            14: ("K", 0, 0), 16: ("K", 0, 1), 18: ("K", 0, 2), 19: ("XT",), 20: ("K", 0, 3), 23: ("Q",),
            25: ("K", 1, 0), 28: ("K", 1, 1), 30: ("K", 1, 2), 33: ("K", 1, 3), 36: ("V", 0), 38: ("V", 1),
            40: ("V", 2), 43: ("V", 3), 45: ("V", 4), 49: ("V", 5), 51: ("V", 6)}
POST0_AT = {5: ("WO", 0), 7: ("WO", 1)}
POST1_AT = {5: ("WO", 0), 7: ("WO", 1), 10: ("HT",), 12: ("FC", 0), 17: ("FC", 1), 27: ("FC", 2), 32: ("FC", 3),
            37: ("PJ", 0), 41: ("PJ", 1)}
APPLY_AT = {0: 0, 1: 1, 4: 2, 5: 3, 7: 4, 8: 5, 11: 6}
STATS_AT = {31: 0, 32: 1, 34: 2, 36: 3, 38: 4, 40: 5, 44: 6}
CTX_LOAD_AT = (43, 23)
FIRST = ([("XT",)] + [("T", k) for k in range(7)] + [("K", 0, c) for c in range(4)]
         + [("Q",), ("V", 0), ("V", 1), ("V", 2), ("V", 3), ("V", 4), ("K", 1, 0), ("K", 1, 1), ("MX", NG), ("V", 5),
            ("K", 1, 2), ("K", 1, 3), ("V", 6)])
FIRST_CHUNKS = {("MX", NG): range(16), ("V", 5): range(16, 18), ("K", 1, 2): range(18, 20),
                ("K", 1, 3): range(20, 21), ("V", 6): range(21, 16 + EARLY)}
FETCHES = ((slice(0, 8), 2), (slice(8, 12), 3), (slice(12, 16), 4))


class Block:

    def __init__(self, n0, i, prep, prep_b, post, post_b):
        self.n0, self.i, self.par = n0, i, n0 % 2
        self.n = n0 + 2 * i
        self.prep, self.prep_b, self.post, self.post_b = prep, prep_b, post, post_b
        self.attends = 0 <= n0 < 16
        at = {}
        if self.attends:
            at.update({u: m for u, m in MAXIMA_AT.items() if n0 < 15 or m[1] < NG})
        if n0 < 0:
            at.update(enumerate(FIRST))
        for more in ({None: {}, 0: {0: PREP0_FIRST_AT, 2: PREP0_AT}.get(n0, {}), 1: PREP1_AT}[prep],
                     {None: {}, 0: POST0_AT, 1: POST1_AT}[post]):
            assert not set(at) & set(more)
            at.update(more)
        self.pieces = [at[u] for u in sorted(at)]
        self.at = {u: at[u] for u in sorted(at)}
        self.misc0 = 0

    def misc(self, piece):
        return self.misc0 + self.pieces.index(piece)

    def outstanding(self, piece):
        if self.attends:
            return 0
        saver = [{"K": 0, "Q": 0, "WO": 0, "PJ": 0, "MX": 0, "XT": 1, "HT": 1}.get(p[0], 2) for p in self.pieces]
        at = n = self.pieces.index(piece)
        while n and saver[n - 1] == saver[at]:
            n -= 1
        return min(at - n, 2)

    def group(self, g):
        return 4 * self.n + g

    def split(self, o):
        return 9 * (self.n + 1) + o

    def split_ever(self, o):
        return self.n0 >= 0 or o >= 2

    def split_buffer(self, o):
        return (9 * (self.n0 + 1) + o) % 2

    def split_uses(self, o):
        return 9 * self.i + (9 * (self.n0 + 1) + o) // 2

    def uses_through(self, o, buf):
        s = 9 * (self.n0 + 1) + o
        last = s if s % 2 == buf else s - 1
        return 9 * self.i + last // 2 + 1


ORDER = {-1: (0, 0, None, 0), 0: (0, 1, None, 0), 1: (1, 0, 0, 0), 2: (0, 2, 0, 1), 3: (1, 1, 1, 0),
         14: (1, 7, 0, 7), 15: (None, 0, 1, 6), 16: (None, 0, 1, 7)}


def make_block(n0, i):
    prep, pb, post, qb = ORDER[n0]
    at_zero = {n: Block(n, 0, *ORDER[n]) for n in ORDER}
    count = {n: len(b.pieces) for n, b in at_zero.items()}
    blk = Block(n0, i, prep, pb + i, post, qb + i)
    per_loop = count[2] + count[3]
    if n0 <= 3:
        blk.misc0 = sum(count[n] for n in range(-1, n0)) + per_loop * i
    else:
        blk.misc0 = sum(count[n] for n in range(-1, 2)) + per_loop * LOOPS + sum(count[n] for n in range(14, n0))
    return blk


def walk(engine, visit):
    for n0 in (-1, 0, 1):
        visit(make_block(n0, 0))
    with engine.Fori(0, LOOPS) as i:
        for n0 in (2, 3):
            visit(make_block(n0, i))
    for n0 in (14, 15, 16):
        visit(make_block(n0, 0))


def split_no(piece):
    return 4 if piece[0] == "Q" else piece[2] + 5 * piece[1]


def chunk_cols(c):
    return 4 * P if c < 3 else LAST


def unit_chunks(blk, u):
    if blk.n0 < 0:
        return [(NG + c // 16, c % 16) for c in FIRST_CHUNKS.get(blk.at[u], ())]
    if not blk.attends:
        return []
    doubles = DOUBLES[blk.prep == 1]
    first = 16 + EARLY + u + sum(d < u for d in doubles)
    every = range(first, first + 1 + (u in doubles))
    return [(c // 16, c % 16) for c in every if blk.n0 < 15 or c // 16 < NG]


def tile_pair(k):
    return range(2 * k, min(2 * k + 2, NT))


def tile_rows(j):
    return P if j < NT - 1 else LAST


def build(nc, x, ctx, mask, Wq0, Wk0, Wv0, Wo0, gamma0, beta0, gate, ln1_w, ln1_b, q_w, q_b, k_w, k_b, v_w, v_b,
          o_w, o_b, ln2_w, ln2_b, fc_w, fc_b, pj_w, pj_b, out):
    scr_k = nc.dram_tensor("scr_k", [CH, 3, P, S], BF16, kind="Internal").ap()
    scr_q = nc.dram_tensor("scr_q", [3, CH, P, T], BF16, kind="Internal").ap()
    scr_max = nc.dram_tensor("scr_max", [2, 3 * HG * TT, P], BF16, kind="Internal").ap()
    scr_mask = nc.dram_tensor("scr_mask", [B, S], BF16, kind="Internal").ap()
    scr_ones = nc.dram_tensor("scr_ones", [P, 3 * 8], BF16, kind="Internal").ap()
    scr_vb = nc.dram_tensor("scr_vb", [D], F32, kind="Internal").ap()
    scr_row = nc.dram_tensor("scr_row", [2, D], F32, kind="Internal").ap()

    es = ExitStack()
    with es:
        def sb(name, shape, dt=F32):
            return es.enter_context(nc.sbuf_tensor(name, shape, dt))

        def sem(name):
            return es.enter_context(nc.semaphore(name))

        wq = [sb(f"wq{l}", [P, CH, D]) for l in range(2)]
        wk = [sb(f"wk{l}", [P, CH, D]) for l in range(2)]
        wv = [sb(f"wv{l}", [P, CH, D]) for l in range(2)]
        wo = [sb(f"wo{l}", [P, NG, D]) for l in range(2)]
        wfc = sb("wfc", [P, CH, FF])
        wpj = sb("wpj", [P, FT, D])
        pj_bias = sb("pj_bias", [P, D])
        ident = sb("ident", [P, P])
        ident_h = sb("ident_h", [P, P], BF16)
        cols = sb("cols", [P, 42])
        c_g0, c_b0, c_w1, c_b1, c_w2, c_b2 = (cols[:, 2 * k:2 * k + 2] for k in range(6))
        kbias = [cols[:, 12:14], cols[:, 14:16]]
        qbias = [cols[:, 16:18], cols[:, 18:20]]
        ln_eps_col, one_col = cols[:, 38:39], cols[:, 41:42]
        tgate, neg_half = cols[:, 20:21], cols[:, 21:22]
        fcbias = cols[:, 22:30]
        vb_pad = [cols[:, 30:34], cols[:, 34:38]]
        bias_row = sb("bias_row", [1, 2, D])

        ctxn = sb("ctxn", [P, NT, D])
        ctxt = sb("ctxt", [P, NT, CH, P])
        vals = [sb(f"vals{k}", [P, NT, H, VW]) for k in range(2)]
        parts = [sb(f"parts{k}", [P, 3, 4 * P], BF16) for k in range(2)]
        rest = sb("rest", [P, 2, 4 * P])
        kst = sb("kst", [RB, H, S], BF16)
        qst = sb("qst", [RB, H, T], BF16)
        prob = sb("prob", [P, 2, HG, T])
        maxes = sb("maxes", [P, 16])
        neg_max = sb("neg_max", [P, 8])
        max_parts = sb("max_parts", [P, 3, 8], BF16)
        max_rows = sb("max_rows", [3 * 8, P], BF16)
        o_raw = sb("o_raw", [P, T])
        o_den = sb("o_den", [P, T])
        o_t = sb("o_t", [P, NG, T])
        xin = [sb(f"xin{k}", [P, TT, D]) for k in range(2)]
        x1 = sb("x1", [P, TT, D])
        x1_kept = sb("x1_kept", [P, TT, D])
        normed = sb("normed", [P, TT, D])
        x_t = sb("x_t", [P, CH, T])
        hid = sb("hid", [P, TT, D])
        z = sb("z", [P, 2, T])
        z2 = sb("z2", [P, 2, T])
        g_t = sb("g_t", [P, FT, T])
        y = sb("y", [P, TT, D])
        st = sb("st", [P, NT, 6])
        mv = sb("mv", [P, NT, 2])
        rstd = sb("rstd", [P, NT])
        st2 = sb("st2", [P, TT, 6])
        mv2 = sb("mv2", [P, TT, 2])
        rstd2 = sb("rstd2", [P, TT])
        mask_u = g_t[0:B, 0:2, :].rearrange("b a c -> b (a c)").bitcast(mybir.dt.uint8)[:, 0:S]
        mask_h = g_t[0:B, 2:6, :].rearrange("b a c -> b (a c)").bitcast(BF16)[:, 0:S]

        p_sc = es.enter_context(nc.psum_tensor("p_sc", [P, 2, 512], F32))
        p_mx = es.enter_context(nc.psum_tensor("p_mx", [P, 2, 2, 512], F32))
        p_acc = es.enter_context(nc.psum_tensor("p_acc", [P, 512], F32))
        p_misc = es.enter_context(nc.psum_tensor("p_misc", [P, 512], F32))

        raw_loaded = sem("raw_loaded")
        loaded = sem("loaded")
        mask_in = sem("mask_in")
        ones_out = sem("ones_out")
        ones_in = sem("ones_in")
        w_padded = sem("w_padded")
        const_made = sem("const_made")
        w_turned = sem("w_turned")
        w_saved = sem("w_saved")
        bias_summed = sem("bias_summed")
        bias_saved = sem("bias_saved")
        folded = sem("folded")
        vb_moved = sem("vb_moved")
        row_summed = sem("row_summed")
        row_saved = sem("row_saved")
        rows_placed = sem("rows_placed")
        gate_ready = sem("gate_ready")
        mask_made = sem("mask_made")
        mask_stored = sem("mask_stored")
        pool_step = sem("pool_step")
        dve_step = sem("dve_step")
        scores_ready = sem("scores_ready")
        exp_done = sem("exp_done")
        chunk_ready = sem("chunk_ready")
        chunk_done = sem("chunk_done")
        weighed = sem("weighed")
        acc_saved = sem("acc_saved")
        den_step = sem("den_step")
        o_ready = sem("o_ready")
        max_step = sem("max_step")
        max_split = sem("max_split")
        max_out = sem("max_out")
        max_in = sem("max_in")
        misc_ready = sem("misc_ready")
        misc_saved = sem("misc_saved")
        high_ready = sem("high_ready")
        mid_ready = sem("mid_ready")
        low_ready = sem("low_ready")
        parts_out = [sem(f"parts_out{k}") for k in range(2)]
        k_in = [sem(f"k_in{k}") for k in range(3)]
        q_in = [sem(f"q_in{k}") for k in range(3)]
        ctx_in = sem("ctx_in")
        x_in = sem("x_in")
        ctx_stats = sem("ctx_stats")
        ctx_var = sem("ctx_var")
        ctx_eps = sem("ctx_eps")
        ctx_rstd = sem("ctx_rstd")
        ctx_normed = sem("ctx_normed")
        ln_stats = [sem(f"ln_stats{k}") for k in range(2)]
        ln_var = [sem(f"ln_var{k}") for k in range(2)]
        ln_eps = [sem(f"ln_eps{k}") for k in range(2)]
        ln_rstd = [sem(f"ln_rstd{k}") for k in range(2)]
        ln_done = [sem(f"ln_done{k}") for k in range(2)]
        kept = sem("kept")
        hid_biased = sem("hid_biased")
        square_done = sem("square_done")
        square_ready = sem("square_ready")
        cube_ready = sem("cube_ready")
        tanh_done = sem("tanh_done")
        tanh_ready = sem("tanh_ready")
        gelu_ready = sem("gelu_ready")
        y_out = sem("y_out")

        block = es.enter_context(nc.Block())

        raw = ctxt[:, :, :, :].rearrange("p a b c -> p (a b c)")
        raw_qkv = [raw[:, 512 * k:512 * k + 512].rearrange("p (c i) -> p c i", c=CH) for k in range(3)]
        raw_o = raw[:, 1536:2560].rearrange("p (c g q d) -> p c g q d", c=CH, g=NG, q=HG)
        raw_wo = raw[:, 2560:3072].rearrange("p (c i) -> p c i", c=CH)
        LOADED, RAW_LOADED = 16 * (7 + 5 + 2 * HG + 3), 16 * 6
        early_ones = max_parts

        def hold(engine, signal, value):
            if not isinstance(value, int):
                value = engine.to_reg(value)
            engine.wait_ge(const_made, 1)
            engine.wait_ge(signal, value)

        def attended_batch(blk):
            return {0: 0, 1: 1, 2: blk.i, 3: blk.i + 2, 14: 6, 15: 7}[blk.n0]

        def next_ctx(blk):
            if blk.n0 == 3:
                j = blk.i + 3
                return (j - j // B).with_bounds(min_val=2, max_val=B - 1)
            return {-1: 1, 0: 0, 1: 2, 2: blk.i + 1}[blk.n0]

        def next_prep_b(blk):
            return blk.i + (2 if blk.n0 == 1 else 3)

        def ctx_load(sp, blk_b, after_misc):
            if after_misc is not None:
                hold(sp, misc_ready, after_misc)
            sp.dma_start(ctxn[:, 0:NT - 1, :], ctx[blk_b, 0:FULL, :].rearrange("(p j) d -> p j d", j=NT - 1)
                         ).then_inc(ctx_in, 16)
            sp.dma_start(ctxn[0:LAST, NT - 1, :], ctx[blk_b, FULL:S, :]).then_inc(ctx_in, 16)

        @block.sync
        def _(sp):
            for dst, w in (*zip(raw_qkv, (Wq0, Wk0, Wv0)), (raw_wo, Wo0)):
                sp.dma_start(dst, w.rearrange("(c o) i -> o c i", o=P)).then_inc(raw_loaded, 16)
            sp.wait_ge(const_made, 1)
            ctx_load(sp, 0, None)
            with nc.allow_non_contiguous_dma(reason="feature vectors as columns, once"):
                for dst, src in ((c_g0, gamma0), (c_b0, beta0)):
                    sp.dma_start(dst, src.rearrange("(c p) -> p c", p=P)).then_inc(raw_loaded, 16)
                sp.dma_start(xin[0][:, :, :], x[0].rearrange("(p t) d -> p t d", t=TT)).then_inc(x_in, 16)
                sp.wait_ge(const_made, 2)
                sp.dma_start(scr_ones, early_ones[:, :, :].rearrange("p k a -> p (k a)")).then_inc(ones_out, 16)
                sp.wait_ge(ones_out, 16)
                ones = scr_ones.rearrange("p a -> (p a)")
                sp.dma_start(kst[RA:RB, :, :], ones[0:S].unsqueeze(0).unsqueeze(0).broadcast_to([RB - RA, H, S])
                             ).then_inc(ones_in, 16)
                sp.dma_start(qst[RP:RA, :, :], ones[0:T].unsqueeze(0).unsqueeze(0).broadcast_to([1, H, T])
                             ).then_inc(ones_in, 16)
                for dst, src in ((c_w1, ln1_w), (c_b1, ln1_b), (c_w2, ln2_w), (c_b2, ln2_b), (kbias[1], k_b),
                                 (qbias[1], q_b), (fcbias, fc_b)):
                    sp.dma_start(dst, src.rearrange("(c p) -> p c", p=P)).then_inc(loaded, 16)
            sp.wait_ge(const_made, 10)
            with nc.allow_non_contiguous_dma(reason="a bias spread over the heads' rows, once"):
                for q in range(HG):
                    sp.dma_start(wo[1][32 * q:32 * q + DH, :, :],
                                  o_w.rearrange("(g q d) e -> q d g e", q=HG, d=DH)[q]).then_inc(loaded, 16)
                    sp.dma_start(vb_pad[1][32 * q:32 * q + DH, :],
                                  v_b.rearrange("(g q d) -> q d g", q=HG, d=DH)[q]).then_inc(loaded, 16)
            sp.dma_start(pj_bias[:, :], pj_b.unsqueeze(0).broadcast_to([P, D])).then_inc(loaded, 16)
            sp.dma_start(tgate, gate.unsqueeze(0).broadcast_to([P, 1])).then_inc(loaded, 16)
            sp.dma_start(hid[0:1, 0, :], o_b.unsqueeze(0)).then_inc(loaded, 16)
            sp.wait_ge(mask_made, 1)
            sp.dma_start(scr_mask, mask_h).then_inc(mask_stored, 16)
            sp.wait_ge(bias_saved, 3)
            sp.wait_ge(const_made, 10)
            with nc.allow_non_contiguous_dma(reason="a vector from columns, once"):
                sp.dma_start(scr_vb.rearrange("(c p) -> p c", p=P), cols[:, 39:41]).then_inc(vb_moved, 16)
                sp.wait_ge(vb_moved, 16)
                for q in range(HG):
                    sp.dma_start(vb_pad[0][32 * q:32 * q + DH, :],
                                 scr_vb.rearrange("(g q d) -> q d g", q=HG, d=DH)[q]).then_inc(vb_moved, 16)
            sp.wait_ge(mask_stored, 16)

            def place_bias_rows():
                sp.wait_ge(row_saved, 2)
                for l in range(2):
                    sp.dma_start(wo[l][DH:DH + 1, 0, :], bias_row[:, l, :]).then_inc(rows_placed, 16)

            def split_out(blk, piece):
                o = split_no(piece)
                buf = blk.split_buffer(o)
                first = blk.n0 < 0
                hold(sp, low_ready, blk.split(o) + 1)
                if piece[0] == "Q":
                    if not first:
                        for k in range(3):
                            hold(sp, q_in[k], 96 * (blk.n + 1))
                    sp.dma_start(scr_q.rearrange("k m r t -> r k m t"),
                                 parts[buf][:, :, :].rearrange("r k (m t) -> r k m t", m=CH)
                                 ).then_inc(parts_out[buf], 16)
                else:
                    m, c = piece[1:]
                    if not first:
                        for k in ((0,), (1, 2))[m]:
                            hold(sp, k_in[k], 112 * (blk.n + 1))
                    w = chunk_cols(c)
                    sp.dma_start(scr_k[m].rearrange("k r s -> r k s")[:, :, 512 * c:512 * c + w],
                                 parts[buf][:, :, 0:w]).then_inc(parts_out[buf], 16)

            def fetch_keys(n, blk, k, blk_b, first):
                hs, groups = FETCHES[k]
                for buf in range(2):
                    hold(sp, parts_out[buf], 16 * blk.uses_through(3 if k == 0 else 8, buf))
                if not first:
                    hold(sp, scores_ready, 104 * (n - 1) + 26 * groups)
                nh, m = hs.stop - hs.start, hs.start // 8
                rows = slice(DH * hs.start - P * m, DH * hs.stop - P * m)
                for j, (_, kp) in enumerate(PARTS):
                    sp.dma_start(kst[DH * j:DH * j + DH, hs, :], scr_k[m, kp, rows].rearrange("(h d) s -> d h s", d=DH)
                                 ).then_inc(k_in[k], 16)
                sp.dma_start(kst[RP:RP + 1, hs, :], scr_mask[blk_b].unsqueeze(0).unsqueeze(0).broadcast_to([1, nh, S])
                             ).then_inc(k_in[k], 16)

            def fetch_queries(blk, k):
                hs, _ = FETCHES[k]
                for buf in range(2):
                    hold(sp, parts_out[buf], 16 * blk.uses_through(4 if k == 0 else 8, buf))
                m = hs.start // 8
                rows = slice(DH * hs.start - P * m, DH * hs.stop - P * m)
                for j, (qp, _) in enumerate(PARTS):
                    sp.dma_start(qst[DH * j:DH * j + DH, hs, :], scr_q[qp, m, rows].rearrange("(h d) t -> d h t", d=DH)
                                 ).then_inc(q_in[k], 16)

            def maxima_move(blk, g):
                G = blk.group(g)
                slot = g % 2
                hold(sp, misc_saved, blk.misc(("MX", g)) + 1)
                if blk.n0 > 0 or (blk.n0 == 0 and g >= 2):
                    hold(sp, max_in, 16 * (G - 1))
                sp.dma_start(scr_max[slot], max_rows[:, :]).then_inc(max_out, 16)
                hold(sp, max_out, 16 * (G + 1))
                heads = slice(HG * (g % NG), HG * (g % NG) + HG)
                sp.dma_start(qst[RA:RB, heads, :].rearrange("k h t -> k (h t)"),
                             scr_max[slot].rearrange("(k a) t -> k (a t)", k=3)).then_inc(max_in, 16)

            def visit(blk):
                n = blk.n
                if blk.n0 == 0:
                    place_bias_rows()
                if 0 <= blk.n0 < 16:
                    maker = Block(blk.n0 - 1, blk.i, None, 0, None, 0)
                    fetch_keys(n, maker, 2, attended_batch(blk), blk.n0 == 0)
                    fetch_queries(maker, 2)
                if blk.n0 == 0:
                    sp.dma_start(xin[1][:, :, :], x[1].rearrange("(p t) d -> p t d", t=TT)).then_inc(x_in, 16)
                units = range(UNITS) if blk.attends else [u for u in blk.at]
                for u in units:
                    piece = blk.at.get(u)
                    kind = piece[0] if piece else None
                    if kind in ("K", "Q"):
                        split_out(blk, piece)
                    if piece == ("WO", 1) and blk.post == 0 and blk.prep == 0:
                        hold(sp, misc_saved, blk.misc(piece) + 1)
                        sp.dma_start(xin[1][:, :, :], x[blk.prep_b].rearrange("(p t) d -> p t d", t=TT)
                                     ).then_inc(x_in, 16)
                    if kind == "MX":
                        if blk.post == 1 and piece[1] == NG:
                            hold(sp, y_out, 16 * (blk.post_b + 1))
                        maxima_move(blk, piece[1])
                    if blk.n0 < 14 and (u == CTX_LOAD_AT[blk.par] if blk.attends else piece == ("K", 1, 1)):
                        ctx_load(sp, next_ctx(blk), blk.misc(("T", NT // 2)) + 1)
                    if piece == ("PJ", 1):
                        hold(sp, misc_saved, blk.misc(piece) + 1)
                        sp.dma_start(out[blk.post_b].rearrange("(p t) d -> p t d", t=TT), y[:, :, :]
                                     ).then_inc(y_out, 16)
                    if blk.prep is not None and (u == 26 if blk.attends else piece == ("K", 0, 3)):
                        fetch_keys(n + 1, blk, 0, blk.prep_b, blk.n0 < 0)
                    if blk.prep is not None and (u == 26 if blk.attends else piece == ("Q",)):
                        fetch_queries(blk, 0)
                    if blk.prep is not None and (u == 40 if blk.attends else piece == ("K", 1, 3)):
                        fetch_keys(n + 1, blk, 1, blk.prep_b, blk.n0 < 0)
                        fetch_queries(blk, 1)

            walk(sp, visit)
            sp.wait_ge(y_out, 16 * B)

        def kept_at(blk, prep):
            return xin[0] if blk.n0 == (14 if prep == 1 else 16) else x1_kept

        def gelu_buffers(blk, k):
            if blk.attends:
                return z[:, :, :], z2[:, :, :]
            own = (z[:, :, :], z2[:, :, :], *(rest[:, i, :].rearrange("p (a t) -> p a t", a=2) for i in range(2)))
            return prob[:, k // 2, 2 * (k % 2):2 * (k % 2) + 2, :], own[k]

        def bank(blk, piece):
            at = 0 if blk.attends else blk.pieces.index(piece) % 3
            return p_misc[:, :] if at == 0 else p_sc[:, at - 1, :]

        def gelu_steps(blk, u, after):
            units = list(range(UNITS)) if blk.attends else list(blk.at)
            back = units.index(u) - ((1, 2, 3, 4) if blk.attends else (0, 0, 1, 1))[after]
            piece = blk.at.get(units[back]) if back >= 0 and blk.post == 1 else None
            return [piece[1]] if piece and piece[0] == "FC" else []

        def ctx_apply(engine, blk, js):
            if js[0] == 0:
                hold(engine, ctx_rstd, blk.prep_b + 1)
            for j in js:
                engine.tensor_scalar(ctxn[:, j, :], ctxn[:, j, :], mv[:, j, 0:1], rstd[:, j:j + 1],
                                     ALU.subtract, ALU.mult).then_inc(ctx_normed, 1)

        @block.gpsimd
        def _(pool):
            pool.memset(ctxn[:, NT - 1, :], 0.0).then_inc(const_made, 1)
            pool.memset(early_ones[:, :, :], 1.0).then_inc(const_made, 1)
            pool.memset(ident[:, :], 0.0).then_inc(pool_step, 1)
            pool.memset(ident_h[:, :], 0.0).then_inc(pool_step, 1)
            pool.memset(one_col, 1.0).then_inc(pool_step, 1)
            pool.wait_ge(pool_step, 3)
            for t in (ident, ident_h):
                pool.affine_select(out=t[:, :], in_=t[:, :], compare_op=ALU.not_equal, fill=1.0, base=0,
                                   pattern=[[-1, P]], channel_multiplier=1).then_inc(const_made, 1)
            pool.memset(raw[:, 1536:2560], 0.0).then_inc(const_made, 1)
            pool.memset(ln_eps_col, LN_EPS).then_inc(pool_step, 1)
            pool.memset(neg_half, -0.5).then_inc(const_made, 1)
            for l in range(2):
                pool.memset(wo[l][:, :, :], 0.0).then_inc(const_made, 1)
            for l in range(2):
                pool.memset(vb_pad[l], 0.0).then_inc(const_made, 1)
            for k in range(2):
                pool.memset(vals[k][:, :, :, DH], 1.0).then_inc(const_made, 1)
            pool.wait_ge(pool_step, 4)
            pool.wait_ge(const_made, 12)

            def split_low(blk, piece):
                o = split_no(piece)
                s, buf = blk.split(o), blk.split_buffer(o)
                w = chunk_cols(piece[2]) if piece[0] == "K" else 512
                pool.wait_ge(mid_ready, s + 1)
                pool.tensor_tensor(parts[buf][:, 2, 0:w], rest[:, buf, 0:w], parts[buf][:, 1, 0:w], ALU.subtract
                                   ).then_inc(low_ready, 1)

            def inverse_root(var, dst, b, var_sem, eps_sem, out_sem):
                pool.wait_ge(var_sem, b + 1)
                pool.tensor_tensor(dst, var, ln_eps_col.broadcast_to(list(dst.shape)), ALU.add).then_inc(eps_sem, 1)
                pool.wait_ge(eps_sem, b + 1)
                pool.tensor_tensor(dst, dst, neg_half.broadcast_to(list(dst.shape)), ALU.pow).then_inc(out_sem, 1)

            def cube(blk, k):
                hold(pool, square_ready, 4 * blk.post_b + k + 1)
                pool.tensor_tensor(z2[:, :, :], z2[:, :, :], z[:, :, :], ALU.mult).then_inc(cube_ready, 1)

            def gelu(blk, k):
                hold(pool, tanh_ready, 4 * blk.post_b + k + 1)
                pool.tensor_tensor(g_t[:, 2 * k:2 * k + 2, :], z2[:, :, :], z[:, :, :], ALU.mult).then_inc(gelu_ready, 1)

            def output(G, g):
                pool.wait_ge(den_step, 3 * G + 3)
                pool.tensor_tensor(o_t[:, g, :], o_raw[:, :], o_den[:, :], ALU.mult).then_inc(o_ready, 1)

            def visit(blk):
                units = range(UNITS) if blk.attends else [-1] + [u for u in blk.at]
                if blk.n0 == 16:
                    output(blk.group(0) - 1, NG - 1)
                for u in units:
                    piece = blk.at.get(u)
                    if blk.prep == 0 and blk.n0 < 2 and u == (7 if blk.attends else -1):
                        inverse_root(mv[:, :, 1], rstd[:, :], blk.prep_b, ctx_var, ctx_eps, ctx_rstd)
                    if blk.n0 in (1, 3) and u == max(STATS_AT) + 2:
                        inverse_root(mv[:, :, 1], rstd[:, :], next_prep_b(blk), ctx_var, ctx_eps, ctx_rstd)
                    if blk.prep == 1 and u == 10:
                        inverse_root(mv2[:, :, 1], rstd2[:, :], blk.prep_b, ln_var[0], ln_eps[0], ln_rstd[0])
                    if blk.prep == 1 and u == 11:
                        pool.tensor_copy(kept_at(blk, blk.prep)[:, :, :], x1[:, :, :]).then_inc(kept, 1)
                    if blk.post == 1 and piece == ("WO", 1):
                        inverse_root(mv2[:, :, 1], rstd2[:, :], blk.post_b, ln_var[1], ln_eps[1], ln_rstd[1])
                        pool.wait_ge(ln_done[1], blk.post_b + 1)
                        pool.tensor_tensor(hid[:, :, :], hid[:, :, :],
                                           pj_bias[:, :].unsqueeze(1).broadcast_to([P, TT, D]), ALU.add
                                           ).then_inc(hid_biased, 1)
                    if blk.n0 == 0 and 8 <= u <= 14:
                        ctx_apply(pool, blk, tile_pair(u - 8))
                    if blk.n0 == 2 and u in APPLY_AT:
                        ctx_apply(pool, blk, tile_pair(APPLY_AT[u]))
                    if blk.attends:
                        for k in gelu_steps(blk, u, 3):
                            gelu(blk, k)
                        for k in gelu_steps(blk, u, 1):
                            cube(blk, k)
                    if blk.attends and u % NT == 2 and (blk.n0 > 0 or u >= NT):
                        output(blk.group(u // NT) - 1, (u // NT - 1) % NG)
                    if piece and piece[0] in ("K", "Q"):
                        split_low(blk, piece)

            walk(pool, visit)

        @block.scalar
        def _(act):
            act.dma_start(mask_u, mask).then_inc(mask_in, 16)
            for k, (dst, src) in enumerate(((wk[0], p_sc[:, 0, :]), (wv[0], p_sc[:, 1, :]), (wq[0], p_mx[:, 0, 0, :]),
                                            (wo[0][:, 0:2, :], p_mx[:, 0, 1, :]), (wo[0][:, 2:4, :], p_mx[:, 1, 0, :]))):
                act.wait_ge(w_turned, k + 1)
                if k == 3:
                    act.wait_ge(const_made, 7)
                dst = dst if k > 2 else dst[:, :, :]
                act.activation(dst.rearrange("p c o -> p (c o)"), src, ACT.Copy).then_inc(w_saved, 1)
            for w, src in ((wq[1], q_w), (wk[1], k_w), (wv[1], v_w)):
                act.dma_start(w[:, :, :], src.rearrange("(c i) o -> i c o", i=P)).then_inc(loaded, 16)
            act.dma_start(wfc[:, :, :], fc_w.rearrange("(c i) o -> i c o", i=P)).then_inc(loaded, 16)
            act.dma_start(wpj[:, :, :], pj_w.rearrange("(f i) o -> i f o", i=P)).then_inc(loaded, 16)
            def save_piece(blk, piece):
                kind, m, res = piece[0], blk.misc(piece), bank(blk, piece)
                act.wait_ge(misc_ready, m + 1)
                if kind == "T":
                    k = piece[1]
                    if k < NT // 2:
                        act.activation(ctxt[:, 2 * k:2 * k + 2, :, :].rearrange("p j c s -> p (j c s)"),
                                       res, ACT.Copy).then_inc(misc_saved, 1)
                    else:
                        act.activation(ctxt[:, NT - 1, :, 0:LAST],
                                       res[:, 0:2 * P].rearrange("p (c s) -> p c s", c=CH)[:, :, 0:LAST],
                                       ACT.Copy).then_inc(misc_saved, 1)
                elif kind == "K":
                    o, w = split_no(piece), chunk_cols(piece[2])
                    buf = blk.split_buffer(o)
                    if blk.split_ever(o):
                        act.wait_ge(parts_out[buf], 16 * blk.split_uses(o))
                    act.activation(parts[buf][:, 0, 0:w], res[:, 0:w], ACT.Identity,
                                   bias=kbias[blk.prep][:, piece[1]:piece[1] + 1]).then_inc(high_ready, 1)
                elif kind == "Q":
                    buf = blk.split_buffer(4)
                    act.wait_ge(parts_out[buf], 16 * blk.split_uses(4))
                    for c in range(CH):
                        ins = act.activation(parts[buf][:, 0, T * c:T * c + T], res[:, T * c:T * c + T],
                                             ACT.Identity, bias=qbias[blk.prep][:, c:c + 1])
                    ins.then_inc(high_ready, 1)
                elif kind == "V":
                    k = piece[1]
                    dst = vals[1 - blk.par]
                    if k == 0 and blk.n0 >= 1:
                        act.wait_ge(weighed, UNITS * blk.n)
                    rows = tile_rows(2 * k)
                    js = slice(2 * k, min(2 * k + 2, NT))
                    nj = js.stop - js.start
                    act.activation(dst[0:rows, js, :, 0:DH],
                                   res[0:rows, 0:D * nj].rearrange("p (j h d) -> p j h d", j=nj, h=H),
                                   ACT.Copy).then_inc(misc_saved, 1)
                elif kind in ("XT", "HT"):
                    act.activation((y if kind == "XT" else x_t)[:, :, :].rearrange("p c t -> p (c t)"), res,
                                   ACT.Copy).then_inc(misc_saved, 1)
                elif kind == "FC":
                    k, b = piece[1], blk.post_b
                    zk, _ = gelu_buffers(blk, k)
                    if k and blk.attends:
                        act.wait_ge(gelu_ready, 4 * b + k)
                    for a in range(2):
                        f = 2 * k + a
                        ins = act.activation(zk[:, a, :], res[:, T * a:T * a + T], ACT.Identity,
                                             bias=fcbias[:, f:f + 1])
                    ins.then_inc(misc_saved, 1)

            def square(blk, k):
                zk, tk = gelu_buffers(blk, k)
                act.wait_ge(misc_saved, blk.misc(("FC", k)) + 1)
                if not blk.attends:
                    act.activation(tk, zk, ACT.Square).then_inc(square_ready, 1)
                    return
                act.activation(tk, zk, ACT.Square).then_inc(square_done, 1)
                act.wait_ge(square_done, 4 * blk.post_b + k + 1)
                act.activation(tk, tk, ACT.Identity, bias=one_col, scale=GELU_B).then_inc(square_ready, 1)

            def tanh(blk, k):
                _, tk = gelu_buffers(blk, k)
                act.wait_ge(cube_ready, 4 * blk.post_b + k + 1)
                if not blk.attends:
                    act.activation(tk, tk, ACT.Tanh, scale=GELU_A * GELU_B).then_inc(tanh_ready, 1)
                    return
                act.activation(tk, tk, ACT.Tanh, scale=GELU_A).then_inc(tanh_done, 1)
                act.wait_ge(tanh_done, 4 * blk.post_b + k + 1)
                act.activation(tk, tk, ACT.Identity, bias=one_col).then_inc(tanh_ready, 1)

            def exps(blk, u):
                j, rows = u % NT, tile_rows(u % NT)
                for half in range(2):
                    k = 104 * blk.n + 2 * u + half
                    act.wait_ge(scores_ready, k + 1)
                    if half == 0 and (blk.n0 > 0 or u >= 2):
                        act.wait_ge(weighed, UNITS * blk.n + u - 1)
                    act.activation(prob[0:rows, u % 2, 2 * half:2 * half + 2, :].rearrange("p h t -> p (h t)"),
                                   p_sc[0:rows, half, :], ACT.Exp).then_inc(exp_done, 1)

            def save_sums(G, through):
                act.wait_ge(weighed, through)
                if not isinstance(G, int) or G:
                    act.wait_ge(o_ready, G)
                act.activation(o_raw[:, :], p_acc[:, 0:T], ACT.Copy).then_inc(acc_saved, 1)

            def visit(blk):
                units = range(UNITS) if blk.attends else list(blk.at)
                if blk.n0 == 16:
                    save_sums(blk.group(0) - 1, UNITS * blk.n)
                for u in units:
                    if blk.attends:
                        exps(blk, u)
                    if blk.attends and u % NT == 0 and (blk.n0 > 0 or u):
                        g = u // NT
                        save_sums(blk.group(g) - 1, UNITS * blk.n + u)
                    piece = blk.at.get(u)
                    if blk.attends:
                        for k in gelu_steps(blk, u, 2):
                            tanh(blk, k)
                        for k in gelu_steps(blk, u, 0):
                            square(blk, k)
                    if piece and piece[0] not in ("MX", "WO", "PJ"):
                        save_piece(blk, piece)
                    if not blk.attends and piece:
                        for k in gelu_steps(blk, u, 0):
                            square(blk, k)
                        for k in gelu_steps(blk, u, 2):
                            tanh(blk, k)
                    if blk.n0 < 0 and piece == ("Q",):
                        act.wait_ge(loaded, LOADED)
                        act.activation(tgate, tgate, ACT.Tanh).then_inc(gate_ready, 1)

            walk(act, visit)

        @block.vector
        def _(dve):
            dve.memset(p_acc[:, :], 0.0).then_inc(dve_step, 1)
            dve.wait_ge(raw_loaded, RAW_LOADED)
            dve.wait_ge(const_made, 5)
            dve.tensor_copy(raw_o.rearrange("p c g q d -> p (c g q) d")[:, :, 0:DH],
                            raw_wo.rearrange("p c (h d) -> p (c h) d", d=DH)).then_inc(w_padded, 1)
            dve.wait_ge(mask_in, 16)
            for src, dst in ((mask_u[:, 0:FULL].rearrange("b (p j) -> b j p", j=NT - 1),
                              mask_h[:, 0:FULL].rearrange("b (j p) -> b j p", j=NT - 1)),
                             (mask_u[:, FULL:S], mask_h[:, FULL:S])):
                ins = dve.tensor_scalar(dst, src, -1.0, -MASKED, ALU.add, ALU.mult)
            ins.then_inc(mask_made, 1)
            scale = float(DH) ** -0.5

            def fold_first():
                dve.wait_ge(bias_summed, 1)
                dve.tensor_copy(kbias[0], p_misc[:, 0:2]).then_inc(bias_saved, 1)
                dve.memset(qbias[0], 0.0).then_inc(bias_saved, 1)
                dve.tensor_copy(cols[:, 39:41], p_misc[:, 2:4]).then_inc(bias_saved, 1)
                dve.wait_ge(w_saved, 3)
                for c in range(CH):
                    for w in (wk[0], wv[0]):
                        dve.tensor_scalar(w[:, c, :], w[:, c, :], c_g0[:, c:c + 1], None, ALU.mult
                                          ).then_inc(folded, 1)
                    dve.tensor_scalar(wq[0][:, c, :], wq[0][:, c, :], scale, None, ALU.mult).then_inc(folded, 1)

            def fold_second():
                dve.wait_ge(loaded, LOADED)
                dve.wait_ge(bias_summed, 2)
                dve.tensor_tensor(qbias[1], p_acc[:, T:T + 2], qbias[1], ALU.add).then_inc(bias_saved, 1)
                dve.tensor_tensor(fcbias, p_acc[:, T + 2:T + 10], fcbias, ALU.add).then_inc(bias_saved, 1)
                dve.wait_ge(bias_saved, 5)
                dve.tensor_scalar(qbias[1], qbias[1], scale, None, ALU.mult).then_inc(folded, 1)
                for c in range(CH):
                    dve.tensor_scalar(wq[1][:, c, :], wq[1][:, c, :], c_w1[:, c:c + 1], scale, ALU.mult, ALU.mult
                                      ).then_inc(folded, 1)
                    dve.tensor_scalar(wfc[:, c, :], wfc[:, c, :], c_w2[:, c:c + 1], None, ALU.mult
                                      ).then_inc(folded, 1)
                dve.wait_ge(row_summed, 1)
                dve.tensor_copy(bias_row[:, 0, :], p_mx[0:1, 0, 0, 0:D]).then_inc(row_saved, 1)
                dve.tensor_tensor(bias_row[:, 1, :], p_mx[0:1, 0, 1, 0:D], hid[0:1, 0, :], ALU.add
                                  ).then_inc(row_saved, 1)

            def reduce_chunk(blk, g, c):
                k = 16 * blk.group(g) + c
                dve.wait_ge(chunk_ready, k + 1)
                dve.tensor_reduce(maxes[:, c:c + 1], p_mx[:, c % 2, :, 0:CW], AX.XY, ALU.max).then_inc(chunk_done, 1)
                if c == 15:
                    split_maxima(blk.group(g))

            def split_maxima(G):
                dve.wait_ge(chunk_done, 16 * (G + 1))
                dve.tensor_reduce(neg_max[:, :], maxes[:, :].rearrange("p (a b) -> p a b", b=2), AX.X, ALU.max,
                                  negate=True).then_inc(max_step, 1)
                dve.wait_ge(max_step, 4 * G + 1)
                dve.tensor_copy(max_parts[:, 0, :], neg_max[:, :]).then_inc(max_step, 1)
                dve.wait_ge(max_step, 4 * G + 2)
                dve.tensor_tensor(neg_max[:, :], neg_max[:, :], max_parts[:, 0, :], ALU.subtract).then_inc(max_step, 1)
                dve.wait_ge(max_step, 4 * G + 3)
                dve.tensor_copy(max_parts[:, 1, :], neg_max[:, :]).then_inc(max_step, 1)
                dve.wait_ge(max_step, 4 * G + 4)
                dve.tensor_tensor(max_parts[:, 2, :], neg_max[:, :], max_parts[:, 1, :], ALU.subtract
                                  ).then_inc(max_split, 1)

            def divide(G, g, step):
                if step == 0:
                    hold(dve, acc_saved, G + 1)
                    dve.stream_shuffle(o_den[:, :], o_raw[:, :], [DH] * 32).then_inc(den_step, 1)
                    return
                half = slice(P * (step - 1), P * step)
                dve.wait_ge(den_step, 3 * G + 1)
                dve.reciprocal(o_den[:, half], o_den[:, half]).then_inc(den_step, 1)

            def ctx_stat_tiles(blk, js, ahead):
                if js[0] == 0:
                    dve.wait_ge(ctx_in, 32 * (blk.n + 1 + ahead))
                    if blk.n0 < 0:
                        dve.wait_ge(const_made, 1)
                for j in js:
                    ins = dve.bn_stats(st[:, j, :], ctxn[:, j, :])
                if js[-1] == NT - 1:
                    ins.then_inc(ctx_stats, 1)

            def ctx_var_all(b):
                hold(dve, ctx_stats, b + 1)
                for j in range(NT):
                    ins = dve.bn_aggr(mv[:, j, :], st[:, j, :])
                ins.then_inc(ctx_var, 1)

            def ln_rows(k, src, b):
                for t in range(TT):
                    ins = dve.bn_stats(st2[:, t, :], src[:, t, :])
                ins.then_inc(ln_stats[k], 1)
                hold(dve, ln_stats[k], b + 1)
                for t in range(TT):
                    ins = dve.bn_aggr(mv2[:, t, :], st2[:, t, :])
                ins.then_inc(ln_var[k], 1)

            def ln_apply(k, src, b):
                dve.wait_ge(ln_rstd[k], b + 1)
                for t in range(TT):
                    ins = dve.tensor_scalar(normed[:, t, :], src[:, t, :], mv2[:, t, 0:1], rstd2[:, t:t + 1],
                                            ALU.subtract, ALU.mult)
                ins.then_inc(ln_done[k], 1)

            def do_piece(blk, piece):
                kind, m, res = piece[0], blk.misc(piece), bank(blk, piece)
                if kind == "MX":
                    dve.wait_ge(misc_ready, m + 1)
                    if blk.n0 >= 0:
                        dve.wait_ge(max_out, 16 * blk.group(piece[1]))
                    dve.tensor_copy(max_rows[:, :], res[0:24, 0:P // 2].bitcast(BF16)).then_inc(misc_saved, 1)
                elif kind in ("K", "Q"):
                    o = split_no(piece)
                    s, buf = blk.split(o), blk.split_buffer(o)
                    bias = kbias[blk.prep][:, piece[1]:piece[1] + 1] if kind == "K" else None
                    w = chunk_cols(piece[2]) if kind == "K" else 512
                    dve.wait_ge(high_ready, s + 1)
                    if blk.split_ever(o):
                        dve.wait_ge(low_ready, s - 1)
                    if kind == "K":
                        dve.scalar_tensor_tensor(out=rest[:, buf, 0:w], in0=res[:, 0:w], scalar=bias,
                                                 in1=parts[buf][:, 0, 0:w], op0=ALU.add, op1=ALU.subtract
                                                 ).then_inc(misc_saved, 1)
                    else:
                        for c in range(CH):
                            cs = slice(T * c, T * c + T)
                            ins = dve.scalar_tensor_tensor(out=rest[:, buf, cs], in0=res[:, cs],
                                                           scalar=qbias[blk.prep][:, c:c + 1],
                                                           in1=parts[buf][:, 0, cs], op0=ALU.add, op1=ALU.subtract)
                        ins.then_inc(misc_saved, 1)
                    dve.wait_ge(misc_saved, m + 1)
                    dve.tensor_copy(parts[buf][:, 1, 0:w], rest[:, buf, 0:w]).then_inc(mid_ready, 1)
                elif kind == "WO":
                    t, b = piece[1], blk.post_b
                    dve.wait_ge(misc_ready, m + 1)
                    if blk.post == 0:
                        if t == 0 and blk.n0 != 1:
                            dve.wait_ge(kept, b)
                        if blk.n0 == 1:
                            dve.wait_ge(gate_ready, 1)
                        dve.scalar_tensor_tensor(out=x1[:, t, :], in0=res[:, 0:D], scalar=tgate,
                                                 in1=xin[1 - blk.par][:, t, :], op0=ALU.mult, op1=ALU.add
                                                 ).then_inc(misc_saved, 1)
                    else:
                        if t == 0:
                            dve.wait_ge(kept, b + 1)
                        dve.tensor_tensor(hid[:, t, :], res[:, 0:D], kept_at(blk, None)[:, t, :], ALU.add
                                          ).then_inc(misc_saved, 1)
                        if t == 1:
                            dve.wait_ge(misc_saved, m + 1)
                            ln_rows(1, hid, b)
                elif kind == "PJ":
                    t, b = piece[1], blk.post_b
                    dve.wait_ge(misc_ready, m + 1)
                    if t == 0:
                        dve.wait_ge(hid_biased, b + 1)
                        if blk.n0 == 16:
                            dve.wait_ge(y_out, 16 * b)
                    dve.scalar_tensor_tensor(out=y[:, t, :], in0=res[:, 0:D], scalar=0.5, in1=hid[:, t, :],
                                             op0=ALU.mult, op1=ALU.add).then_inc(misc_saved, 1)

            def visit(blk):
                if not blk.attends and blk.prep == 0:
                    ctx_stat_tiles(blk, range(NT), 1)
                    ctx_var_all(blk.prep_b)
                    fold_first()
                    ctx_apply(dve, blk, range(NT))
                if blk.n0 == 16:
                    for step in range(3):
                        divide(blk.group(0) - 1, NG - 1, step)
                for u in (range(UNITS) if blk.attends else list(blk.at)):
                    piece = blk.at.get(u)
                    cs = unit_chunks(blk, u)
                    if blk.attends and piece and piece[0] == "MX":
                        do_piece(blk, piece)
                    for g, c in cs:
                        reduce_chunk(blk, g, c)
                    divides = blk.attends and (blk.n0 > 0 or u >= NT)
                    if divides and u % NT in (1, 2):
                        divide(blk.group(u // NT) - 1, (u // NT - 1) % NG, u % NT)
                    if blk.n0 == 0:
                        if u <= 6:
                            ctx_stat_tiles(blk, tile_pair(u), 1)
                        if u == 6:
                            ctx_var_all(blk.prep_b)
                    if blk.n0 in (1, 3) and u in STATS_AT:
                        ctx_stat_tiles(blk, tile_pair(STATS_AT[u]), 2)
                    if blk.n0 in (1, 3) and u == max(STATS_AT) + 1:
                        ctx_var_all(next_prep_b(blk))
                    if blk.post == 1 and (u == 8 if blk.attends else piece == ("HT",)):
                        ln_apply(1, hid, blk.post_b)
                    if blk.prep == 1 and u == 10:
                        if blk.post == 1:
                            dve.wait_ge(ln_done[1], blk.post_b + 1)
                        else:
                            dve.wait_ge(misc_saved, blk.misc(("WO", 1)) + 1)
                        ln_rows(0, x1, blk.prep_b)
                    if blk.prep == 1 and u == 13:
                        if blk.post == 1:
                            dve.wait_ge(misc_saved, blk.misc(("HT",)) + 1)
                        ln_apply(0, x1, blk.prep_b)
                    if not blk.attends:
                        for k in gelu_steps(blk, u, 1):
                            zk, tk = gelu_buffers(blk, k)
                            dve.wait_ge(square_ready, 4 * blk.post_b + k + 1)
                            dve.scalar_tensor_tensor(out=tk, in0=tk, scalar=1.0 / GELU_B, in1=zk,
                                                     op0=ALU.add, op1=ALU.mult).then_inc(cube_ready, 1)
                        for k in gelu_steps(blk, u, 3):
                            zk, tk = gelu_buffers(blk, k)
                            dve.wait_ge(tanh_ready, 4 * blk.post_b + k + 1)
                            dve.scalar_tensor_tensor(out=g_t[:, 2 * k:2 * k + 2, :], in0=tk, scalar=1.0, in1=zk,
                                                     op0=ALU.add, op1=ALU.mult).then_inc(gelu_ready, 1)
                    if piece and piece[0] in ("K", "Q", "WO", "PJ") or blk.n0 < 0 and piece[0] == "MX":
                        do_piece(blk, piece)
                    if blk.n0 < 0 and piece == ("Q",):
                        fold_second()
                    if divides and u % NT == 0:
                        divide(blk.group(u // NT) - 1, (u // NT - 1) % NG, 0)

            walk(dve, visit)

        @block.tensor
        def _(pe):
            mm = nc.tensor.matmul
            pe.wait_ge(const_made, 4)
            pe.wait_ge(dve_step, 1)
            pe.wait_ge(raw_loaded, RAW_LOADED)
            for k, dst in ((1, p_sc[:, 0, :]), (2, p_sc[:, 1, :]), (0, p_mx[:, 0, 0, :])):
                for ci in range(CH):
                    for co in range(CH):
                        ins = nc.tensor.transpose(dst[:, D * ci + P * co:D * ci + P * co + P],
                                                  raw_qkv[k][:, co, P * ci:P * ci + P], ident[:, :])
                ins.then_inc(w_turned, 1)
            pe.wait_ge(w_padded, 1)
            for k, dst in enumerate((p_mx[:, 0, 1, :], p_mx[:, 1, 0, :])):
                for g in range(2):
                    for ce in range(CH):
                        ins = nc.tensor.transpose(
                            dst[:, D * g + P * ce:D * g + P * ce + P],
                            raw_o[:, ce, 2 * k + g, :, :].rearrange("p q d -> p (q d)"), ident[:, :])
                ins.then_inc(w_turned, 1)

            def shifts(into, jobs):
                for w, shift, col, nm in jobs:
                    for m in range(nm):
                        for c in range(CH):
                            ins = mm(into[:, col + m:col + m + 1], w[:, c, P * m:P * m + P], shift[:, c:c + 1],
                                     start=(c == 0), stop=(c == CH - 1))
                ins.then_inc(bias_summed, 1)

            pe.wait_ge(w_saved, 2)
            shifts(p_misc, [(wk[0], c_b0, 0, CH), (wv[0], c_b0, 2, CH)])
            pe.wait_ge(bias_saved, 3)
            pe.wait_ge(folded, 3 * CH)

            def second_setup():
                pe.wait_ge(loaded, LOADED)
                shifts(p_acc[:, T:2 * T], [(wq[1], c_b1, 0, CH), (wfc, c_b2, 2, FT)])
                pe.wait_ge(vb_moved, 16 * 5)
                pe.wait_ge(w_saved, 5)
                for l in range(2):
                    for g in range(NG):
                        ins = mm(p_mx[0:1, 0, l, 0:D], vb_pad[l][:, g:g + 1], wo[l][:, g, :],
                                 start=(g == 0), stop=(g == NG - 1))
                ins.then_inc(row_summed, 1)

            def scores(blk, u, half):
                g, j = u // NT, u % NT
                rows = tile_rows(j)
                k = 104 * blk.n + 2 * u + half
                if blk.n0 > 0 or u:
                    pe.wait_ge(exp_done, k - 1)
                elif half == 0:
                    pe.wait_ge(misc_saved, blk.misc0)
                    pe.wait_ge(const_made, 12)
                if half == 0 and j == 0:
                    pe.wait_ge(max_in, 16 * (blk.group(g) + 1))
                for q in range(2):
                    h = HG * g + 2 * half + q
                    ins = mm(p_sc[0:rows, half, T * q:T * q + T], kst[0:RB, h, P * j:P * j + rows],
                             qst[0:RB, h, :], start=True, stop=True)
                ins.then_inc(scores_ready, 1)

            def chunk(blk, g, c):
                k = 16 * blk.group(g) + c
                if blk.n0 >= 0 or g > NG or c >= 2:
                    pe.wait_ge(chunk_done, k - 1)
                elif c == 0:
                    pe.wait_ge(ones_in, 32)
                    pe.wait_ge(row_saved, 2)
                    pe.wait_ge(folded, 3 * CH + 1 + 2 * CH)
                at, gg = (blk.n + 1, g - NG) if g >= NG else (blk.n, g)
                if c == 0 and gg != 1:
                    pe.wait_ge(k_in[max(gg - 1, 0)], 112 * (at + 1))
                    pe.wait_ge(q_in[max(gg - 1, 0)], 96 * (at + 1))
                h, t, half = HG * gg + c // 4, c // 2 % 2, c % 2
                for w in range(2):
                    s0 = 2 * CS * half + CS * w
                    ins = mm(p_mx[:, c % 2, w, 0:CW], qst[0:RA, h, P * t:P * t + P], kst[0:RA, h, s0:s0 + CW],
                             start=True, stop=True)
                ins.then_inc(chunk_ready, 1)

            def weigh(par, units_before, G, u, first):
                g, j = u // NT, u % NT
                rows = tile_rows(j)
                pe.wait_ge(exp_done, 2 * units_before + 2)
                if j == 0 and not first:
                    pe.wait_ge(acc_saved, G)
                for q in range(HG):
                    h = HG * g + q
                    ins = mm(p_acc[32 * q:32 * q + VW, 0:T],
                             vals[par][0:rows, j, h, :], prob[0:rows, u % 2, q, :],
                             start=(j == 0), stop=(j == NT - 1))
                ins.then_inc(weighed, 1)

            def do_piece(blk, piece):
                kind, m, res = piece[0], blk.misc(piece), bank(blk, piece)
                before = m - blk.outstanding(piece)
                if blk.n0 >= 0 or before:
                    pe.wait_ge(misc_saved, before)
                if kind == "T":
                    k = piece[1]
                    js = range(2 * k, min(2 * k + 2, NT))
                    if blk.prep == 0:
                        pe.wait_ge(ctx_normed, NT * blk.prep_b + js[-1] + 1)
                    elif k == 0:
                        pe.wait_ge(ctx_in, 32 * (blk.n + 2))
                    for j in js:
                        r = tile_rows(j)
                        for c in range(CH):
                            o = D * (j - js[0]) + P * c
                            ins = nc.tensor.transpose(res[:, o:o + r], ctxn[0:r, j, P * c:P * c + P],
                                                      ident[0:r, 0:r])
                elif kind == "K":
                    mo, ck = piece[1:]
                    w = chunk_cols(ck)
                    for c in range(CH):
                        rhs = ctxt[:, 4 * ck:4 * ck + 4, c, :] if ck < 3 else ctxt[:, NT - 1, c, 0:LAST]
                        ins = mm(res[:, 0:w], wk[blk.prep][:, c, P * mo:P * mo + P], rhs,
                                 start=(c == 0), stop=(c == CH - 1))
                elif kind == "V":
                    k = piece[1]
                    for j in range(2 * k, min(2 * k + 2, NT)):
                        r, o = tile_rows(j), D * (j % 2)
                        for c in range(CH):
                            ins = mm(res[0:r, o:o + D], ctxt[:, j, c, 0:r], wv[blk.prep][:, c, :],
                                     start=(c == 0), stop=(c == CH - 1))
                elif kind in ("XT", "HT"):
                    if kind == "HT":
                        pe.wait_ge(ln_done[1], blk.post_b + 1)
                        src = normed
                    elif blk.prep == 1:
                        pe.wait_ge(ln_done[0], blk.prep_b + 1)
                        src = normed
                    else:
                        pe.wait_ge(x_in, 16 * (blk.prep_b + 1))
                        src = xin[1 - blk.par]
                    for c in range(CH):
                        for t in range(TT):
                            o = T * c + P * t
                            ins = nc.tensor.transpose(res[:, o:o + P], src[:, t, P * c:P * c + P], ident[:, :])
                elif kind == "Q":
                    for mo in range(CH):
                        for c in range(CH):
                            ins = mm(res[:, T * mo:T * mo + T], wq[blk.prep][:, c, P * mo:P * mo + P],
                                     y[:, c, :], start=(c == 0), stop=(c == CH - 1))
                elif kind == "WO":
                    t = piece[1]
                    pe.wait_ge(o_ready, blk.group(0))
                    pe.wait_ge(rows_placed, 32)
                    for g in range(NG):
                        ins = mm(res[:, 0:D], o_t[:, g, P * t:P * t + P], wo[blk.post][:, g, :],
                                 start=(g == 0), stop=(g == NG - 1))
                elif kind == "FC":
                    for a in range(2):
                        f = 2 * piece[1] + a
                        for c in range(CH):
                            ins = mm(res[:, T * a:T * a + T], wfc[:, c, P * f:P * f + P], x_t[:, c, :],
                                     start=(c == 0), stop=(c == CH - 1))
                elif kind == "PJ":
                    t = piece[1]
                    pe.wait_ge(gelu_ready, 4 * (blk.post_b + 1))
                    for f in range(FT):
                        ins = mm(res[:, 0:D], g_t[:, f, P * t:P * t + P], wpj[:, f, :],
                                 start=(f == 0), stop=(f == FT - 1))
                elif kind == "MX":
                    pe.wait_ge(max_split, blk.group(piece[1]) + 1)
                    ins = nc.tensor.transpose(res[0:24, 0:P // 2].bitcast(BF16),
                                              max_parts[:, :, :].rearrange("p k a -> p (k a)"), ident_h[:, :])
                ins.then_inc(misc_ready, 1)

            def weigh_last_of_before(blk):
                weigh(1 - blk.par, UNITS * blk.n - 1, 0, UNITS - 1, False)

            def visit(blk):
                for u in (range(UNITS) if blk.attends else list(blk.at)):
                    piece = blk.at.get(u)
                    cs = unit_chunks(blk, u)
                    if blk.attends:
                        scores(blk, u, 0)
                        if piece and piece[0] == "MX":
                            do_piece(blk, piece)
                        if cs:
                            chunk(blk, *cs[0])
                        scores(blk, u, 1)
                        if len(cs) > 1:
                            chunk(blk, *cs[1])
                        if piece and piece[0] != "MX":
                            do_piece(blk, piece)
                        if u == 0:
                            if blk.n0 > 0:
                                weigh_last_of_before(blk)
                        else:
                            weigh(blk.par, UNITS * blk.n + u - 1, blk.group((u - 1) // NT), u - 1,
                                  blk.n0 == 0 and u == 1)
                    elif blk.n0 == 16 and u == list(blk.at)[0]:
                        weigh_last_of_before(blk)
                    if not blk.attends:
                        for g, c in cs:
                            chunk(blk, g, c)
                        do_piece(blk, piece)
                        if blk.n0 < 0 and piece == ("Q",):
                            second_setup()

            walk(pe, visit)


_INS = ['x', 'ctx_2048', 'mask_BxS2_bf1', 'L0_xattn_Wq', 'L0_xattn_Wk', 'L0_xattn_Wv', 'L0_xattn_Wo',
        'L0_xattn_ln_gamma', 'L0_xattn_ln_beta', 'L0_xattn_gate', 'L1_xattn_ln1_w', 'L1_xattn_ln1_b', 'L1_xattn_q_w',
        'L1_xattn_q_b', 'L1_xattn_k_w', 'L1_xattn_k_b', 'L1_xattn_v_w', 'L1_xattn_v_b', 'L1_xattn_cproj_w',
        'L1_xattn_cproj_b', 'L1_xattn_ln2_w', 'L1_xattn_ln2_b', 'L1_xattn_fc_w', 'L1_xattn_fc_b', 'L1_xattn_proj_w',
        'L1_xattn_proj_b']


def kernel(**inputs):
    import numpy as _np
    import concourse.bacc as _bacc
    from concourse import mybir as _mybir
    from concourse.bass_utils import run_bass_kernel_spmd as _run

    nc = _bacc.Bacc("TRN2", target_bir_lowering=False, num_devices=1)
    arrays, args = {}, []
    for name in _INS:
        a = _np.ascontiguousarray(inputs[name])
        if a.dtype.kind == "b":
            a = a.view(_np.uint8)
        arrays[f"in_{name}_dram"] = a
        args.append(nc.dram_tensor(f"in_{name}_dram", a.shape, _mybir.dt.from_np(a.dtype), kind="ExternalInput").ap())
    args.append(nc.dram_tensor("out_0_dram", (B, T, D), F32, kind="ExternalOutput").ap())
    build(nc, *args)
    r = _run(nc, [arrays], core_ids=[0])
    return r.results[0]["out_0_dram"]
```
